# Optimizing a Trainium2 kernel written in Bass

```python
import numpy as np
import jax
import jax.numpy as jnp

def _softmax(x, axis=-1):
    return jax.nn.softmax(x, axis=axis)

def _gelu(x):
    return jax.nn.gelu(x, approximate=True)

def _silu(x):
    return jax.nn.silu(x)

def _sigmoid(x):
    return jax.nn.sigmoid(x)

def _layernorm(x, axis=-1, eps=1e-05):
    m = jnp.mean(x, axis=axis, keepdims=True)
    v = jnp.var(x, axis=axis, keepdims=True)
    return (x - m) / jnp.sqrt(v + eps)

def _scatter_add(tgt, idx, src, axis=0):
    return tgt.at[idx].add(src)

def _segment_sum(src, seg, n):
    return jax.ops.segment_sum(src, seg, n)
kernel_name = 'mk_rec_standalone_d1_rec_r8_c05700'

def setup_inputs(seed: int=0):
    np.random.seed(seed)
    _w = jnp.asarray

    def _rec_inputs():
        import jax
        import jax.numpy as jnp
        _rk = jax.random.key(seed)
        r_feat_index = jnp.stack([jax.random.randint(jax.random.fold_in(jax.random.fold_in(_rk, 1), 0), (512,), 128, 999854, jnp.int32), jax.random.randint(jax.random.fold_in(jax.random.fold_in(_rk, 1), 1), (512,), 18, 999393, jnp.int32), jax.random.randint(jax.random.fold_in(jax.random.fold_in(_rk, 1), 2), (512,), 148, 999903, jnp.int32), jax.random.randint(jax.random.fold_in(jax.random.fold_in(_rk, 1), 3), (512,), 200, 999311, jnp.int32), jax.random.randint(jax.random.fold_in(jax.random.fold_in(_rk, 1), 4), (512,), 1, 999794, jnp.int32), jax.random.randint(jax.random.fold_in(jax.random.fold_in(_rk, 1), 5), (512,), 64, 999412, jnp.int32), jax.random.randint(jax.random.fold_in(jax.random.fold_in(_rk, 1), 6), (512,), 6, 999510, jnp.int32), jax.random.randint(jax.random.fold_in(jax.random.fold_in(_rk, 1), 7), (512,), 200, 999878, jnp.int32), jax.random.randint(jax.random.fold_in(jax.random.fold_in(_rk, 1), 8), (512,), 81, 999921, jnp.int32), jax.random.randint(jax.random.fold_in(jax.random.fold_in(_rk, 1), 9), (512,), 341, 999959, jnp.int32), jax.random.randint(jax.random.fold_in(jax.random.fold_in(_rk, 1), 10), (512,), 145, 999174, jnp.int32), jax.random.randint(jax.random.fold_in(jax.random.fold_in(_rk, 1), 11), (512,), 403, 999909, jnp.int32), jax.random.randint(jax.random.fold_in(jax.random.fold_in(_rk, 1), 12), (512,), 92, 999937, jnp.int32), jax.random.randint(jax.random.fold_in(jax.random.fold_in(_rk, 1), 13), (512,), 679, 999945, jnp.int32), jax.random.randint(jax.random.fold_in(jax.random.fold_in(_rk, 1), 14), (512,), 3, 999785, jnp.int32), jax.random.randint(jax.random.fold_in(jax.random.fold_in(_rk, 1), 15), (512,), 62, 999689, jnp.int32), jax.random.randint(jax.random.fold_in(jax.random.fold_in(_rk, 1), 16), (512,), 71, 999716, jnp.int32), jax.random.randint(jax.random.fold_in(jax.random.fold_in(_rk, 1), 17), (512,), 441, 999883, jnp.int32), jax.random.randint(jax.random.fold_in(jax.random.fold_in(_rk, 1), 18), (512,), 978, 999449, jnp.int32), jax.random.randint(jax.random.fold_in(jax.random.fold_in(_rk, 1), 19), (512,), 23, 999437, jnp.int32), jax.random.randint(jax.random.fold_in(jax.random.fold_in(_rk, 1), 20), (512,), 49, 999715, jnp.int32), jax.random.randint(jax.random.fold_in(jax.random.fold_in(_rk, 1), 21), (512,), 158, 999991, jnp.int32), jax.random.randint(jax.random.fold_in(jax.random.fold_in(_rk, 1), 22), (512,), 11, 999779, jnp.int32), jax.random.randint(jax.random.fold_in(jax.random.fold_in(_rk, 1), 23), (512,), 436, 999500, jnp.int32), jax.random.randint(jax.random.fold_in(jax.random.fold_in(_rk, 1), 24), (512,), 29, 999811, jnp.int32), jax.random.randint(jax.random.fold_in(jax.random.fold_in(_rk, 1), 25), (512,), 21, 124982, jnp.int32), jax.random.randint(jax.random.fold_in(jax.random.fold_in(_rk, 1), 26), (512,), 39, 999483, jnp.int32), jax.random.randint(jax.random.fold_in(jax.random.fold_in(_rk, 1), 27), (512,), 131, 999906, jnp.int32), jax.random.randint(jax.random.fold_in(jax.random.fold_in(_rk, 1), 28), (512,), 232, 999509, jnp.int32), jax.random.randint(jax.random.fold_in(jax.random.fold_in(_rk, 1), 29), (512,), 30, 998972, jnp.int32), jax.random.randint(jax.random.fold_in(jax.random.fold_in(_rk, 1), 30), (512,), 39, 124968, jnp.int32), jax.random.randint(jax.random.fold_in(jax.random.fold_in(_rk, 1), 31), (512,), 275, 999919, jnp.int32), jax.random.randint(jax.random.fold_in(jax.random.fold_in(_rk, 1), 32), (512,), 28, 999409, jnp.int32), jax.random.randint(jax.random.fold_in(jax.random.fold_in(_rk, 1), 33), (512,), 171, 999881, jnp.int32), jax.random.randint(jax.random.fold_in(jax.random.fold_in(_rk, 1), 34), (512,), 363, 999826, jnp.int32), jax.random.randint(jax.random.fold_in(jax.random.fold_in(_rk, 1), 35), (512,), 135, 999604, jnp.int32), jax.random.randint(jax.random.fold_in(jax.random.fold_in(_rk, 1), 36), (512,), 276, 999885, jnp.int32), jax.random.randint(jax.random.fold_in(jax.random.fold_in(_rk, 1), 37), (512,), 444, 999830, jnp.int32), jax.random.randint(jax.random.fold_in(jax.random.fold_in(_rk, 1), 38), (512,), 42, 999317, jnp.int32)], axis=1)
        return r_feat_index
    r_feat_index = _rec_inputs()

    def _L0_rec_setup():
        import jax, jax.numpy as jnp
        import numpy as np
        B, F, D = (512, 39, 16)
        V = 125000
        H1, H2 = (128, 128)
        INPUT_DIM = F * D
        FC_DIM = H1 // 2 + H2
        DEEP = [400, 400]
        BN_EPS = 1e-05

        def _bn(x, g, b):
            m = x.mean(axis=0)
            v = x.var(axis=0)
            return g * (x - m) * jax.lax.rsqrt(v + BN_EPS) + b
        key = jax.random.key(seed)
        ks = jax.random.split(key, 16)
        xav = lambda k, shp: jax.random.normal(k, shp, jnp.float32) * np.sqrt(2.0 / (shp[0] + shp[-1]))
        return {'feat_index': jax.random.randint(ks[0], (B, F), 0, V), 'feat_value': jax.random.uniform(ks[1], (B, F), jnp.float32), 'emb_table': xav(ks[2], (V, D)), 'linear_w': xav(ks[3], (INPUT_DIM, 1)), 'linear_b': jnp.zeros((1,), jnp.float32), 'conv_w1': xav(ks[4], (H1, F, F)), 'conv_b1': jnp.zeros((H1,), jnp.float32), 'conv_w2': xav(ks[5], (H2, H1 // 2, F)), 'conv_b2': jnp.zeros((H2,), jnp.float32), 'deep_w1': xav(ks[6], (INPUT_DIM, DEEP[0])), 'deep_b1': jnp.zeros((DEEP[0],), jnp.float32), 'bn_g1': jnp.ones((DEEP[0],), jnp.float32), 'bn_b1': jnp.zeros((DEEP[0],), jnp.float32), 'deep_w2': xav(ks[7], (DEEP[0], DEEP[1])), 'deep_b2': jnp.zeros((DEEP[1],), jnp.float32), 'bn_g2': jnp.ones((DEEP[1],), jnp.float32), 'bn_b2': jnpp if False else jnp.zeros((DEEP[1],), jnp.float32), 'out_w': xav(ks[8], (1 + FC_DIM + DEEP[1], 1)), 'out_b': jnp.zeros((1,), jnp.float32)}
    _L0_rec_all = _L0_rec_setup()
    _L0_rec_in = {k: v for k, v in _L0_rec_all.items() if k in ('feat_value', 'emb_table', 'linear_w', 'linear_b', 'conv_w1', 'conv_b1', 'conv_w2', 'conv_b2', 'deep_w1', 'deep_b1', 'bn_g1', 'bn_b1', 'deep_w2', 'deep_b2', 'bn_g2', 'bn_b2', 'out_w', 'out_b')}
    del _L0_rec_all
    return {'r_feat_index': r_feat_index, 'L0_rec_feat_value': _L0_rec_in['feat_value'], 'L0_rec_emb_table': _L0_rec_in['emb_table'], 'L0_rec_linear_w': _L0_rec_in['linear_w'], 'L0_rec_linear_b': _L0_rec_in['linear_b'], 'L0_rec_conv_w1': _L0_rec_in['conv_w1'], 'L0_rec_conv_b1': _L0_rec_in['conv_b1'], 'L0_rec_conv_w2': _L0_rec_in['conv_w2'], 'L0_rec_conv_b2': _L0_rec_in['conv_b2'], 'L0_rec_deep_w1': _L0_rec_in['deep_w1'], 'L0_rec_deep_b1': _L0_rec_in['deep_b1'], 'L0_rec_bn_g1': _L0_rec_in['bn_g1'], 'L0_rec_bn_b1': _L0_rec_in['bn_b1'], 'L0_rec_deep_w2': _L0_rec_in['deep_w2'], 'L0_rec_deep_b2': _L0_rec_in['deep_b2'], 'L0_rec_bn_g2': _L0_rec_in['bn_g2'], 'L0_rec_bn_b2': _L0_rec_in['bn_b2'], 'L0_rec_out_w': _L0_rec_in['out_w'], 'L0_rec_out_b': _L0_rec_in['out_b']}

def reference(r_feat_index, L0_rec_feat_value, L0_rec_emb_table, L0_rec_linear_w, L0_rec_linear_b, L0_rec_conv_w1, L0_rec_conv_b1, L0_rec_conv_w2, L0_rec_conv_b2, L0_rec_deep_w1, L0_rec_deep_b1, L0_rec_bn_g1, L0_rec_bn_b1, L0_rec_deep_w2, L0_rec_deep_b2, L0_rec_bn_g2, L0_rec_bn_b2, L0_rec_out_w, L0_rec_out_b):
    import jax
    import jax.numpy as jnp

    def _L0_rec_ref(feat_index, feat_value, emb_table, linear_w, linear_b, conv_w1, conv_b1, conv_w2, conv_b2, deep_w1, deep_b1, bn_g1, bn_b1, deep_w2, deep_b2, bn_g2, bn_b2, out_w, out_b):
        import jax, jax.numpy as jnp
        import numpy as np
        B, F, D = (512, 39, 16)
        V = 125000
        H1, H2 = (128, 128)
        INPUT_DIM = F * D
        FC_DIM = H1 // 2 + H2
        DEEP = [400, 400]
        BN_EPS = 1e-05

        def _bn(x, g, b):
            m = x.mean(axis=0)
            v = x.var(axis=0)
            return g * (x - m) * jax.lax.rsqrt(v + BN_EPS) + b
        e = emb_table[feat_index]
        flat = e.reshape(e.shape[0], -1)
        linear_part = flat @ linear_w + linear_b
        x0 = e
        h1 = jax.nn.relu(jnp.einsum('bhd,bmd,ohm->bod', x0, x0, conv_w1) + conv_b1[None, :, None])
        nxt, hi1 = jnp.split(h1, 2, axis=1)
        h2 = jax.nn.relu(jnp.einsum('bhd,bmd,ohm->bod', nxt, x0, conv_w2) + conv_b2[None, :, None])
        res = jnp.concatenate([hi1, h2], axis=1).sum(axis=2)
        y = jax.nn.relu(_bn(flat @ deep_w1 + deep_b1, bn_g1, bn_b1))
        y = jax.nn.relu(_bn(y @ deep_w2 + deep_b2, bn_g2, bn_b2))
        cat = jnp.concatenate([linear_part, res, y], axis=1)
        return cat @ out_w + out_b
    y = _L0_rec_ref(r_feat_index, L0_rec_feat_value, L0_rec_emb_table, L0_rec_linear_w, L0_rec_linear_b, L0_rec_conv_w1, L0_rec_conv_b1, L0_rec_conv_w2, L0_rec_conv_b2, L0_rec_deep_w1, L0_rec_deep_b1, L0_rec_bn_g1, L0_rec_bn_b1, L0_rec_deep_w2, L0_rec_deep_b2, L0_rec_bn_g2, L0_rec_bn_b2, L0_rec_out_w, L0_rec_out_b)
    return y

_drawn_inputs = setup_inputs


def setup_inputs(seed=0):
    import zlib

    import numpy as np

    out = dict(_drawn_inputs(seed))
    spreads = {'L0_rec_conv_b1': (0.0, 0.1),
     'L0_rec_conv_b2': (0.0, 0.1),
     'L0_rec_deep_b1': (0.0, 2.0),
     'L0_rec_bn_g1': (1.0, 0.2),
     'L0_rec_bn_b1': (0.0, 0.1),
     'L0_rec_deep_b2': (0.0, 2.0),
     'L0_rec_bn_g2': (1.0, 0.2),
     'L0_rec_bn_b2': (0.0, 0.1)}
    factors = {'L0_rec_linear_w': 200.0, 'L0_rec_conv_w1': 200.0, 'L0_rec_conv_w2': 8.0}
    for name, (base, spread) in spreads.items():
        noise = np.random.default_rng([zlib.crc32(name.encode()), seed]).standard_normal(out[name].shape)
        drawn = base * np.exp(spread * noise) if base else spread * noise
        out[name] = jnp.asarray(drawn.astype(out[name].dtype))
    for name, factor in factors.items():
        out[name] = (out[name] * factor).astype(out[name].dtype)
    return out
```

```python
import concourse.bass as bass
from concourse import mybir
from contextlib import ExitStack


BATCH, FIELDS, DIM, VOCAB = 512, 39, 16, 125000
H1, H2 = 128, 128
NEXT = H1 // 2
HIDDEN = 400
FLAT = FIELDS * DIM
BN_EPS = 1e-5

ROWS = 128
TILES = BATCH // ROWS
TOK = 1024
HALF_D = TOK // ROWS
BLOCKS = BATCH * DIM // TOK
BANK = 512
CHUNKS = TOK // BANK

OFFSETS = [[3 * t + 1, 3 * t + 2, 3 * t + 3] for t in range(6)] + [[19, 0]]
L1_TILES = len(OFFSETS)
L2_PAIRS = FIELDS // 2
TAIL = L2_PAIRS
L2_ORDER = [TAIL] + list(range(L2_PAIRS))
L2_TILES = len(L2_ORDER)
PER_STEP = L1_TILES + L2_TILES
RING = 9
SPLIT_RING = 4

L1_SPLIT = [1, 3, 5]
L2_SPLIT = [TAIL, 1, 3, 5, 7, 9, 11, 13, 15]
SPLITS_PER_STEP = len(L1_SPLIT) + len(L2_SPLIT)
assert PER_STEP % RING == 0 and SPLITS_PER_STEP % SPLIT_RING == 0

L1_SEQ = [(1, t) for t in range(L1_TILES)]
L2_SEQ = [(2, t) for t in L2_ORDER]
SEQ = L1_SEQ + (L1_SEQ + L2_SEQ) * (BLOCKS - 1) + L2_SEQ

FLAT_K = 104
FLAT_T = FLAT // FLAT_K
HID_K = 100
HID_T = HIDDEN // HID_K


def is_split(tile):
    layer, t = tile
    return t in (L1_SPLIT if layer == 1 else L2_SPLIT)


def loads_of(tile):
    layer, t = tile
    return len(OFFSETS[t]) if layer == 1 else 2


def rows_of(tile):
    layer, t = tile
    return FIELDS * len(OFFSETS[t]) if layer == 1 else 128


def splits_before(s):
    return sum(is_split(x) for x in SEQ[:s])


def seq_of_split(q):
    return [s for s, x in enumerate(SEQ) if is_split(x)][q]


def loads_landed(s):
    return 16 * sum(loads_of(SEQ[r]) for r in range(s % RING, s + 1, RING))


def first_of_l1(j):
    return 0 if j == 0 else L1_TILES + PER_STEP * (j - 1)


def first_of_l2(j):
    return first_of_l1(j + 1) + (L1_TILES if j < BLOCKS - 1 else 0)


def build(nc, idx, emb, lin_w, lin_b, w1a, w1b, b1, w2, b2, dw1, db1, g1, be1, dw2, db2, g2, be2,
          ow_lin, ow_hi, ow_h2, ow_y, ob, out):
    F32, F32R, I32 = mybir.dt.float32, mybir.dt.float32r, mybir.dt.int32
    ALU, ACT, AX = mybir.AluOpType, mybir.ActivationFunctionType, mybir.AxisListType

    xs = nc.dram_tensor("xs_scratch", [2 * FIELDS, BATCH * DIM], F32).ap()

    ctx = ExitStack()
    with ctx:
        def sb(name, shape, dt=F32):
            return ctx.enter_context(nc.sbuf_tensor(name, shape, dt))

        def ps(name, shape, dt=F32):
            return ctx.enter_context(nc.psum_tensor(name, shape, dt))

        def sem(name):
            return ctx.enter_context(nc.semaphore(name))

        idx_raw = sb("idx_raw", [ROWS, TILES, FIELDS], I32)
        idx_wrap = sb("idx_wrap", [ROWS, TILES, FIELDS], F32)
        idx_all = sb("idx_all", [ROWS, TILES, FIELDS], I32)
        idx_cur = sb("idx_cur", [ROWS, FIELDS], I32)
        G = sb("G", [ROWS, FLAT])
        ident = sb("ident", [128, 128])
        xT = sb("xT", [FIELDS, DIM * ROWS])
        flatT = sb("flatT", [FLAT_K, FLAT_T, BATCH])
        ring = sb("ring", [128, RING, TOK])
        zh = sb("zh", [128, SPLIT_RING, TOK], F32R)
        zl = sb("zl", [128, SPLIT_RING, TOK], F32R)
        xa = sb("xa", [3 * FIELDS, 2, TOK])
        nx = sb("nx", [128, 2, TOK])
        hi = sb("hi", [128, TOK])
        h2s = sb("h2s", [128, TOK])
        hi_sum = sb("hi_sum", [128, 2, TILES, ROWS])
        h2_sum = sb("h2_sum", [128, 2, TILES, ROWS])
        w1s = sb("w1s", [3 * FIELDS, L1_TILES, H1])
        w1b_sb = sb("w1b_sb", [3 * FIELDS, L1_TILES, H1])
        w2s = sb("w2s", [128, L2_TILES, H2])
        w1h = sb("w1h", [3 * FIELDS, len(L1_SPLIT), H1], F32R)
        w1l = sb("w1l", [3 * FIELDS, len(L1_SPLIT), H1], F32R)
        w2h = sb("w2h", [128, len(L2_SPLIT), H2], F32R)
        w2l = sb("w2l", [128, len(L2_SPLIT), H2], F32R)
        b1_sb = sb("b1_sb", [H1, 1])
        b1_dup = sb("b1_dup", [128, 1])
        b2_sb = sb("b2_sb", [H2, 1])
        dw1_sb = sb("dw1_sb", [FLAT_K, FLAT_T, HIDDEN])
        dw2_sb = sb("dw2_sb", [HID_K, HID_T, HIDDEN])
        vec = sb("vec", [HID_K, 6, HID_T])
        lw_sb = sb("lw_sb", [FLAT_K, FLAT_T])
        lb_sb = sb("lb_sb", [1, 1])
        pre = sb("pre", [HID_K, HID_T, BATCH])
        act = sb("act", [HID_K, HID_T, BATCH])
        stats = sb("stats", [HID_K, 6])
        mv = sb("mv", [HID_K, 2])
        bn = sb("bn", [HID_K, 8])
        scale = sb("scale", [HID_K, 2 * HID_T])
        shift = sb("shift", [HID_K, 2 * HID_T])
        ow_lin_sb = sb("ow_lin_sb", [1, 1])
        ow_hi_sb = sb("ow_hi_sb", [128, 1])
        ow_h2_sb = sb("ow_h2_sb", [H2, 1])
        ow_y_sb = sb("ow_y_sb", [HID_K, HID_T])
        ob_sb = sb("ob_sb", [1, 1])
        lin = sb("lin", [1, BATCH])
        res = sb("res", [1, BATCH])

        p_h1 = ps("p_h1", [H1, TOK])
        p_h2 = ps("p_h2", [H2, TOK])
        p_t = [ps(f"p_t{i}", [128, BANK]) for i in range(2)]
        p_d = [ps(f"p_d{i}", [128, BANK]) for i in range(2)]

        s_idx = sem("s_idx")
        s_clamp = sem("s_clamp")
        s_w = sem("s_w")
        s_small = sem("s_small")
        s_ident = sem("s_ident")
        s_cur = sem("s_cur")
        s_gather = sem("s_gather")
        s_sym = sem("s_sym")
        s_wh = sem("s_wh")
        s_wl = sem("s_wl")
        s_tp = sem("s_tp")
        s_te = sem("s_te")
        s_xs = [sem(f"s_xs{c}") for c in range(2)]
        s_load = [sem(f"s_load{r}") for r in range(RING)]
        s_xa = [sem(f"s_xa{p}") for p in range(2)]
        s_xa_free = sem("s_xa_free")
        s_z = sem("s_z")
        s_zh = sem("s_zh")
        s_zl = sem("s_zl")
        s_used = sem("s_used")
        s_n = sem("s_n")
        s_n_free = sem("s_n_free")
        s_hi = sem("s_hi")
        s_hi_sum = sem("s_hi_sum")
        s_h2 = sem("s_h2")
        s_h2_sum = sem("s_h2_sum")
        s_dp = sem("s_dp")
        s_pre = sem("s_pre")
        s_bn = sem("s_bn")
        s_root = sem("s_root")
        s_coef = sem("s_coef")
        s_act = sem("s_act")
        s_lin_p = sem("s_lin_p")
        s_lin = sem("s_lin")
        s_acc = sem("s_acc")
        s_res = sem("s_res")
        s_out = sem("s_out")

        s_past = sem("s_past")

        def own_wait(eng, semaphore, value):
            eng.wait_ge(semaphore, value)
            eng.sem_inc(s_past, 1)

        block = ctx.enter_context(nc.Block())

        TP_GROUPS = DIM // 4 + FLAT_T // 3
        T_AT = 8

        def steps(eng, step):
            step(0, 0)
            with eng.Fori(0, 2) as bt:
                step(1, bt)
                step(2, bt)
            for j in range(5, BLOCKS):
                step(j, 0)

        @block.sync
        def _(sp):
            sp.dma_start(idx_raw[:, :, :], idx.rearrange("(t p) f -> p t f", p=ROWS)).then_inc(s_idx, 16)
            sp.dma_start(w1s[:, 0:6, :], w1a[:, 0:6, :]).then_inc(s_w, 16)
            sp.dma_start(w1s[0:78, 6, :], w1a[0:78, 6, :]).then_inc(s_w, 16)
            sp.dma_start(w1b_sb[:, 0:6, :], w1b[:, 0:6, :]).then_inc(s_w, 16)
            sp.dma_start(w1b_sb[0:39, 6, :], w1b[0:39, 6, :]).then_inc(s_w, 16)
            sp.dma_start(w2s[:, 0:L2_PAIRS, :], w2[0:128 * L2_PAIRS, :].rearrange("(t p) o -> p t o", p=128)).then_inc(s_w, 16)
            for half in range(2):
                sp.dma_start(w2s[NEXT * half:NEXT * (half + 1), TAIL, :], w2[128 * L2_PAIRS:, :]).then_inc(s_w, 16)
            sp.dma_start(b1_sb[:, :], b1).then_inc(s_small, 16)
            for half in range(2):
                sp.dma_start(b1_dup[NEXT * half:NEXT * (half + 1), :], b1[0:NEXT, :]).then_inc(s_small, 16)
            sp.dma_start(b2_sb[:, :], b2).then_inc(s_small, 16)
            sp.dma_start(dw1_sb[:, :, :], dw1.rearrange("(t p) o -> p t o", p=FLAT_K)).then_inc(s_small, 16)
            sp.dma_start(dw2_sb[:, :, :], dw2.rearrange("(t p) o -> p t o", p=HID_K)).then_inc(s_small, 16)
            for n, v in enumerate((db1, g1, be1, db2, g2, be2)):
                sp.dma_start(vec[:, n, :], v).then_inc(s_small, 16)
            for dst, src in ((lw_sb, lin_w), (lb_sb, lin_b), (ow_lin_sb, ow_lin), (ow_h2_sb, ow_h2),
                             (ow_y_sb, ow_y), (ob_sb, ob)):
                sp.dma_start(dst[:, :], src).then_inc(s_small, 16)
            sp.dma_start(ow_hi_sb[NEXT:128, :], ow_hi).then_inc(s_small, 16)

            def load_tiles(seq0, j, bt, layer, k):
                col = (j + 2 * bt) * TOK
                if layer == 1:
                    own_wait(sp, s_xs[j % 2], 32 * (j // 2 + 1) + 32 * bt)
                    own_wait(sp, s_xa_free, j + 1 + 2 * bt)
                    for q in range(3):
                        sp.dma_start(xa[FIELDS * q:FIELDS * (q + 1), j % 2, :],
                                     xs[0:FIELDS, bass.ds(col, TOK)]).then_inc(s_xa[j % 2], 16)
                for n, (_, t) in enumerate(L1_SEQ if layer == 1 else L2_SEQ):
                    s = seq0 + n
                    slot = s % RING
                    own_wait(sp, s_used, s + 1 + 2 * PER_STEP * bt)
                    if layer == 1:
                        for q, off in enumerate(OFFSETS[t]):
                            sp.dma_start(ring[FIELDS * q:FIELDS * (q + 1), slot, :],
                                         xs[off:off + FIELDS, bass.ds(col, TOK)]).then_inc(s_load[slot], 16)
                    else:
                        for half in range(2):
                            m = min(2 * t + half, FIELDS - 1)
                            sp.dma_start(ring[NEXT * half:NEXT * (half + 1), slot, :],
                                         xs[m:m + 1, bass.ds(col, TOK)].broadcast_to([NEXT, TOK])).then_inc(s_load[slot], 16)

            load_tiles(0, 0, 0, 1, 0)

            def step(j, bt):
                if j + 1 < BLOCKS:
                    load_tiles(first_of_l1(j + 1), j + 1, bt, 1, 0)
                load_tiles(first_of_l2(j), j, bt, 2, 0)

            steps(sp, step)

            sp.wait_ge(s_res, 1)
            sp.dma_start(out.rearrange("b o -> o b"), res[:, :]).then_inc(s_out, 16)
            sp.wait_ge(s_out, 16)

        @block.gpsimd
        def _(pool):
            def gather():
                for f in range(FIELDS):
                    nc.gpsimd.indirect_dma_start(
                        G[:, DIM * f:DIM * (f + 1)], None, emb[:, :],
                        bass.IndirectOffsetOnAxis(idx_cur[:, f:f + 1], 0)).then_inc(s_gather, 16)

            pool.wait_ge(s_clamp, 3)
            nc.gpsimd.tensor_copy(idx_cur[:, :], idx_all[:, 0, :]).then_inc(s_cur, 1)
            pool.wait_ge(s_cur, 1)
            gather()
            nc.gpsimd.memset(ident[:, :], 0.0).then_inc(s_ident, 1)
            pool.wait_ge(s_ident, 1)
            nc.gpsimd.affine_select(out=ident[:, :], in_=ident[:, :], compare_op=ALU.not_equal, fill=1.0,
                                    base=0, pattern=[[-1, 128]], channel_multiplier=1).then_inc(s_ident, 1)
            with pool.Fori(1, TILES) as t:
                own_wait(pool, s_tp, TP_GROUPS * t)
                nc.gpsimd.tensor_copy(idx_cur[:, :], idx_all[:, bass.ds(t, 1), :].rearrange("p a f -> p (a f)")).then_inc(s_cur, 1)
                own_wait(pool, s_cur, t + 1)
                gather()

        @block.vector
        def _(dve):
            nc.vector.sem_inc(s_xa_free, 2)
            dve.wait_ge(s_idx, 16)
            nc.vector.tensor_scalar(idx_wrap[:, :, :], idx_raw[:, :, :], 0.0, float(VOCAB), ALU.is_lt, ALU.mult).then_inc(s_clamp, 1)
            dve.wait_ge(s_clamp, 1)
            nc.vector.tensor_tensor(idx_wrap[:, :, :], idx_wrap[:, :, :], idx_raw[:, :, :], ALU.add).then_inc(s_clamp, 1)
            dve.wait_ge(s_clamp, 2)
            nc.vector.tensor_scalar(idx_all[:, :, :], idx_wrap[:, :, :], 0.0, float(VOCAB - 1), ALU.max, ALU.min).then_inc(s_clamp, 1)

            dve.wait_ge(s_w, 7 * 16)
            nc.vector.tensor_tensor(w1s[:, 0:6, :], w1s[:, 0:6, :], w1b_sb[:, 0:6, :], ALU.add).then_inc(s_sym, 1)
            nc.vector.tensor_tensor(w1s[0:39, 6, :], w1s[0:39, 6, :], w1b_sb[0:39, 6, :], ALU.add).then_inc(s_sym, 1)
            dve.wait_ge(s_wh, 1)
            dve.wait_ge(s_sym, 2)
            for n, t in enumerate(L1_SPLIT):
                nc.vector.tensor_tensor(w1l[:, n, :], w1s[:, t, :], w1h[:, n, :].bitcast(F32), ALU.subtract)
            for n, t in enumerate(L2_SPLIT):
                last = nc.vector.tensor_tensor(w2l[:, n, :], w2s[:, t, :], w2h[:, n, :].bitcast(F32), ALU.subtract)
            last.then_inc(s_wl, 1)

            def low_part(s, bt):
                q = splits_before(s)
                dve.wait_ge(s_zh, q + 1 + 2 * SPLITS_PER_STEP * bt)
                if q >= SPLIT_RING:
                    dve.wait_ge(s_used, RING + seq_of_split(q - SPLIT_RING) + 1 + 2 * PER_STEP * bt)
                slot, part, r = s % RING, q % SPLIT_RING, rows_of(SEQ[s])
                if SEQ[s] == (2, TAIL):
                    nc.vector.tensor_tensor(zh[NEXT:128, part, :], ring[NEXT:128, slot, :],
                                            zh[NEXT:128, part, :].bitcast(F32), ALU.subtract).then_inc(s_zl, 1)
                else:
                    nc.vector.tensor_tensor(zl[0:r, part, :], ring[0:r, slot, :],
                                            zh[0:r, part, :].bitcast(F32), ALU.subtract).then_inc(s_zl, 1)

            def products(seq0, j, bt, layer, extras):
                if layer == 1:
                    dve.wait_ge(s_xa[j % 2], 48 * (j // 2 + 1) + 48 * bt)
                else:
                    dve.wait_ge(s_n, j + 1 + 2 * bt)
                tiles = L1_SEQ if layer == 1 else L2_SEQ
                for n, tile in enumerate(tiles):
                    s = seq0 + n
                    slot, r = s % RING, rows_of(tile)
                    per = (loads_landed(s + 2 * PER_STEP) if s + 2 * PER_STEP < len(SEQ) else 0) - loads_landed(s)
                    dve.wait_ge(s_load[slot], loads_landed(s) + (per * bt if per > 0 else 0))
                    by = xa[0:r, j % 2, :] if layer == 1 else nx[:, j % 2, :]
                    last = nc.vector.tensor_tensor(ring[0:r, slot, :], by, ring[0:r, slot, :], ALU.mult).then_inc(s_z, 1)
                    if n and is_split(tiles[n - 1]):
                        low_part(s - 1, bt)
                    if n in extras:
                        extras[n]()
                dve.wait_ge(s_z, seq0 + len(tiles) + 2 * PER_STEP * bt)
                nc.vector.sem_inc(s_xa_free if layer == 1 else s_n_free, 1)

            def sum_d(dst, src, j, bt):
                return nc.vector.tensor_reduce(
                    dst[:, j % 2, bass.ds(j // 2 + bt, 1), :].rearrange("p a b -> p (a b)"),
                    src.rearrange("p (d b) -> p b d", d=HALF_D), AX.X, ALU.add)

            def sum_h2(j, bt):
                dve.wait_ge(s_h2, j + 1 + 2 * bt)
                sum_d(h2_sum[:, :, :, :], h2s[:, :], j, bt).then_inc(s_h2_sum, 1)

            def sum_hi(j, bt):
                dve.wait_ge(s_hi, j + 1 + 2 * bt)
                sum_d(hi_sum[NEXT:128, :, :, :], hi[NEXT:128, :], j, bt).then_inc(s_hi_sum, 1)

            count = [0]

            def chain(ins):
                count[0] += 1
                ins.then_inc(s_bn, 1)
                dve.wait_ge(s_bn, count[0])

            def norm(layer, t):
                n = layer * HID_T + t
                dve.wait_ge(s_pre, n + 1)
                chain(nc.vector.bn_stats(stats[:, :], pre[:, t, :]))
                chain(nc.vector.bn_aggr(mv[:, :], stats[:, :]))
                chain(nc.vector.tensor_scalar(bn[:, 0:1], mv[:, 1:2], BN_EPS, None, ALU.add))
                dve.wait_ge(s_root, n + 1)
                chain(nc.vector.reciprocal(bn[:, 2:3], bn[:, 1:2]))
                chain(nc.vector.scalar_tensor_tensor(bn[:, 3:4], bn[:, 0:1], bn[:, 2:3], bn[:, 1:2], ALU.mult, ALU.add))
                chain(nc.vector.tensor_scalar(bn[:, 4:5], bn[:, 3:4], 0.5, None, ALU.mult))
                chain(nc.vector.reciprocal(bn[:, 5:6], bn[:, 4:5]))
                chain(nc.vector.tensor_tensor(scale[:, n:n + 1], bn[:, 5:6], vec[:, 3 * layer + 1, t:t + 1], ALU.mult))
                chain(nc.vector.tensor_tensor(bn[:, 6:7], mv[:, 0:1], scale[:, n:n + 1], ALU.mult))
                nc.vector.tensor_tensor(shift[:, n:n + 1], vec[:, 3 * layer + 2, t:t + 1], bn[:, 6:7], ALU.subtract).then_inc(s_coef, 1)

            products(0, 0, 0, 1, {})

            def step(j, bt):
                if j + 1 < BLOCKS:
                    products(first_of_l1(j + 1), j + 1, bt, 1,
                             {4: (lambda: sum_h2(j - 1, bt)) if j else (lambda: sum_hi(0, 0))})
                extras = {5: lambda: sum_hi(j + 1, bt)}
                if j == BLOCKS - 2:
                    extras[3] = lambda: dve.wait_ge(s_small, 19 * 16)
                    extras.update({6 + 4 * t: (lambda t=t: norm(0, t)) for t in range(3)})
                if j == BLOCKS - 1:
                    extras = {2: lambda: norm(0, 3), 4: lambda: sum_h2(j - 1, bt)}
                    extras.update({8 + 3 * t: (lambda t=t: norm(1, t)) for t in range(4)})
                products(first_of_l2(j), j, bt, 2, extras)

            steps(dve, step)
            sum_h2(BLOCKS - 1, 0)

        @block.tensor
        def _(pe):
            nc.tensor.sem_inc(s_used, RING)

            def transposes(t, bt):
                own_wait(pe, s_gather, 16 * FIELDS * (t + 1) + 16 * FIELDS * bt)
                by_d = G[:, :].rearrange("p (f d) -> p d f", d=DIM)
                for g in range(TP_GROUPS):
                    n = TP_GROUPS * t + g
                    if n >= 2:
                        own_wait(pe, s_te, n - 1 + TP_GROUPS * bt)
                    bank = p_t[g % 2]
                    if g < DIM // 4:
                        for c in range(4):
                            last = nc.tensor.transpose(bank[0:FIELDS, 128 * c:128 * (c + 1)], by_d[:, 4 * g + c, :], ident[:, :])
                    else:
                        for c in range(3):
                            k = 3 * (g - DIM // 4) + c
                            last = nc.tensor.transpose(bank[0:FLAT_K, 128 * c:128 * (c + 1)],
                                                       G[:, FLAT_K * k:FLAT_K * (k + 1)], ident[:, :])
                    last.then_inc(s_tp, 1)

            def contract(seq0, j, bt, layer, extras):
                acc = p_h1 if layer == 1 else p_h2
                tiles = L1_SEQ if layer == 1 else L2_SEQ
                if layer == 1 and j:
                    pe.wait_ge(s_hi, j + 2 * bt)
                if layer == 2 and j:
                    pe.wait_ge(s_h2, j + 2 * bt)
                for n, tile in enumerate(tiles):
                    s = seq0 + n
                    t, slot, r = tile[1], s % RING, rows_of(tile)
                    first, final = n == 0, n == len(tiles) - 1

                    def mm(c, w, x, start=False, stop=False):
                        return nc.tensor.matmul(acc[:, BANK * c:BANK * (c + 1)], w, x[:, BANK * c:BANK * (c + 1)],
                                                start=start, stop=stop)

                    if not is_split(tile):
                        pe.wait_ge(s_z, s + 1 + 2 * PER_STEP * bt)
                        w = (w1s if layer == 1 else w2s)[0:r, t, :]
                        for c in range(CHUNKS):
                            last = mm(c, w, ring[0:r, slot, :], first, final)
                    else:
                        q = splits_before(s)
                        part = q % SPLIT_RING
                        k = (L1_SPLIT if layer == 1 else L2_SPLIT).index(t)
                        wh, wl = ((w1h, w1l) if layer == 1 else (w2h, w2l))
                        wh, wl = wh[0:r, k, :], wl[0:r, k, :]
                        high, low = zh[0:r, part, :], zl[0:r, part, :]
                        if t == TAIL and layer == 2:
                            pe.wait_ge(s_zl, q + 1 + 2 * SPLITS_PER_STEP * bt)
                            for c in range(CHUNKS):
                                mm(c, wl, high, first)
                            for c in range(CHUNKS):
                                last = mm(c, wh, high, False, final)
                        else:
                            pe.wait_ge(s_zh, q + 1 + 2 * SPLITS_PER_STEP * bt)
                            for c in range(CHUNKS):
                                mm(c, wl, high, first)
                            for c in range(CHUNKS):
                                mm(c, wh, high)
                            pe.wait_ge(s_zl, q + 1 + 2 * SPLITS_PER_STEP * bt)
                            for c in range(CHUNKS):
                                last = mm(c, wh, low, False, final)
                    last.then_inc(s_used, 1)
                    if n in extras:
                        extras[n]()

            def deep(layer, t):
                n = layer * HID_T + t
                if n >= 2:
                    pe.wait_ge(s_pre, n - 1)
                if layer == 0:
                    if t == 0:
                        pe.wait_ge(s_te, TP_GROUPS * TILES)
                        pe.wait_ge(s_small, 19 * 16)
                    src, w, k = flatT, dw1_sb, FLAT_T
                else:
                    if t == 0:
                        pe.wait_ge(s_act, HID_T)
                    src, w, k = act, dw2_sb, HID_T
                for c in range(k):
                    last = nc.tensor.matmul(p_d[n % 2][0:HID_K, :], w[:, c, HID_K * t:HID_K * (t + 1)], src[:, c, :],
                                            start=c == 0, stop=c == k - 1)
                last.then_inc(s_dp, 1)

            def linear():
                for c in range(FLAT_T):
                    last = nc.tensor.matmul(p_t[0][0:1, :], lw_sb[:, c:c + 1], flatT[:, c, :], start=c == 0, stop=c == FLAT_T - 1)
                last.then_inc(s_lin_p, 1)

            pe.wait_ge(s_ident, 2)
            transposes(0, 0)
            pe.wait_ge(s_wl, 1)
            contract(0, 0, 0, 1, {})

            def step(j, bt):
                if j + 1 < BLOCKS:
                    contract(first_of_l1(j + 1), j + 1, bt, 1, {})
                extras = {}
                if j % 2 == 0 and j < BLOCKS - 2:
                    extras = {T_AT: lambda: transposes(j // 2 + 1, bt)}
                if j == BLOCKS - 2:
                    extras = {3 + 4 * t: (lambda t=t: deep(0, t)) for t in range(HID_T)}
                if j == BLOCKS - 1:
                    extras = {5 + 3 * t: (lambda t=t: deep(1, t)) for t in range(HID_T)}
                    extras[2] = linear
                contract(first_of_l2(j), j, bt, 2, extras)

            steps(pe, step)

            total = p_t[1][0:1, :]
            pe.wait_ge(s_lin, 1)
            nc.tensor.matmul(total, ow_lin_sb[:, :], lin[:, :], start=True, stop=False)
            pe.wait_ge(s_hi_sum, BLOCKS)
            for c in range(2):
                nc.tensor.matmul(total, ow_hi_sb[NEXT:128, :], hi_sum[NEXT:128, c, :, :].rearrange("p t b -> p (t b)"), start=False, stop=False)
            pe.wait_ge(s_act, 2 * HID_T)
            for t in range(HID_T):
                nc.tensor.matmul(total, ow_y_sb[:, t:t + 1], act[:, t, :], start=False, stop=False)
            pe.wait_ge(s_h2_sum, BLOCKS)
            for c in range(2):
                last = nc.tensor.matmul(total, ow_h2_sb[:, :], h2_sum[:, c, :, :].rearrange("p t b -> p (t b)"), start=False, stop=c == 1)
            last.then_inc(s_acc, 1)

        @block.scalar
        def _(sc):
            nc.scalar.sem_inc(s_n_free, 2)

            sc.wait_ge(s_sym, 2)
            for n, t in enumerate(L1_SPLIT):
                nc.scalar.activation(w1h[:, n, :], w1s[:, t, :], ACT.Copy)
            for n, t in enumerate(L2_SPLIT):
                last = nc.scalar.activation(w2h[:, n, :], w2s[:, t, :], ACT.Copy)
            last.then_inc(s_wh, 1)

            def out_of_transposes(t, bt):
                for g in range(TP_GROUPS):
                    n = TP_GROUPS * t + g
                    sc.wait_ge(s_tp, n + 1 + TP_GROUPS * bt)
                    if g < DIM // 4:
                        if t and g % 2 == 0:
                            sc.wait_ge(s_xs[g // 2], 32 * t + 32 * bt)
                        nc.scalar.activation(xT[:, BANK * g:BANK * (g + 1)], p_t[g % 2][0:FIELDS, :], ACT.Copy).then_inc(s_te, 1)
                        if g % 2:
                            half = g // 2
                            sc.wait_ge(s_te, n + 1 + TP_GROUPS * bt)
                            for copy in range(2):
                                sc.dma_start(xs[FIELDS * copy:FIELDS * (copy + 1), bass.ds((2 * t + half) * TOK + 2 * TOK * bt, TOK)],
                                             xT[:, TOK * half:TOK * (half + 1)]).then_inc(s_xs[half], 16)
                    else:
                        k = 3 * (g - DIM // 4)
                        nc.scalar.activation(
                            flatT[:, k:k + 3, bass.ds(ROWS * t + ROWS * bt, ROWS)],
                            p_t[g % 2][0:FLAT_K, 0:3 * ROWS].rearrange("p (k b) -> p k b", k=3), ACT.Copy).then_inc(s_te, 1)

            def high_parts(seq0, bt, layer, extras):
                tiles = L1_SEQ if layer == 1 else L2_SEQ
                for n, tile in enumerate(tiles):
                    s = seq0 + n
                    if is_split(tile):
                        q = splits_before(s)
                        sc.wait_ge(s_z, s + 1 + 2 * PER_STEP * bt)
                        if q >= SPLIT_RING:
                            sc.wait_ge(s_used, RING + seq_of_split(q - SPLIT_RING) + 1 + 2 * PER_STEP * bt)
                        r = rows_of(tile)
                        nc.scalar.activation(zh[0:r, q % SPLIT_RING, :], ring[0:r, s % RING, :], ACT.Copy).then_inc(s_zh, 1)
                    if n in extras:
                        extras[n]()

            def out_of_l1(seq_end, j, bt):
                sc.wait_ge(s_used, RING + seq_end + 2 * PER_STEP * bt)
                sc.wait_ge(s_n_free, j + 1 + 2 * bt)
                nc.scalar.activation(nx[0:NEXT, j % 2, :], p_h1[0:NEXT, :], ACT.Relu, bias=b1_dup[0:NEXT, :])
                nc.scalar.activation(nx[NEXT:128, j % 2, :], p_h1[0:NEXT, :], ACT.Relu, bias=b1_dup[NEXT:128, :]).then_inc(s_n, 1)
                if j:
                    sc.wait_ge(s_hi_sum, j + 2 * bt)
                nc.scalar.activation(hi[NEXT:128, :], p_h1[NEXT:128, :], ACT.Relu, bias=b1_sb[NEXT:128, :]).then_inc(s_hi, 1)

            def out_of_l2(seq_end, j, bt):
                sc.wait_ge(s_used, RING + seq_end + 2 * PER_STEP * bt)
                if j:
                    sc.wait_ge(s_h2_sum, j + 2 * bt)
                nc.scalar.activation(h2s[:, :], p_h2[:, :], ACT.Relu, bias=b2_sb[:, :]).then_inc(s_h2, 1)

            def deep_bias(layer, t):
                n = layer * HID_T + t
                sc.wait_ge(s_dp, n + 1)
                if layer:
                    sc.wait_ge(s_act, HID_T)
                nc.scalar.activation(pre[:, t, :], p_d[n % 2][0:HID_K, :], ACT.Identity, bias=vec[:, 3 * layer, t:t + 1]).then_inc(s_pre, 1)

            def deep_root(n):
                sc.wait_ge(s_bn, 9 * n + 3)
                nc.scalar.activation(bn[:, 1:2], bn[:, 0:1], ACT.Sqrt).then_inc(s_root, 1)

            def deep_act(layer, t):
                n = layer * HID_T + t
                sc.wait_ge(s_coef, n + 1)
                if layer and t == 0:
                    sc.wait_ge(s_dp, 2 * HID_T)
                nc.scalar.activation(act[:, t, :], pre[:, t, :], ACT.Relu, bias=shift[:, n:n + 1],
                                     scale=scale[:, n:n + 1]).then_inc(s_act, 1)

            def linear():
                sc.wait_ge(s_lin_p, 1)
                nc.scalar.activation(lin[:, :], p_t[0][0:1, :], ACT.Identity, bias=lb_sb[:, :]).then_inc(s_lin, 1)

            out_of_transposes(0, 0)
            high_parts(0, 0, 1, {})
            sc.wait_ge(s_small, 19 * 16)
            out_of_l1(L1_TILES, 0, 0)

            def step(j, bt):
                if j + 1 < BLOCKS:
                    high_parts(first_of_l1(j + 1), bt, 1, {})
                    out_of_l1(first_of_l1(j + 1) + L1_TILES, j + 1, bt)
                extras = {}
                if j % 2 == 0 and j < BLOCKS - 2:
                    extras = {T_AT: lambda: out_of_transposes(j // 2 + 1, bt)}
                if j == BLOCKS - 2:
                    extras = {3 + 4 * t: (lambda t=t: deep_bias(0, t)) for t in range(HID_T)}
                    extras.update({6 + 4 * t: (lambda t=t: (deep_root(t), deep_act(0, t))) for t in range(3)})
                if j == BLOCKS - 1:
                    extras = {2: lambda: (deep_root(3), deep_act(0, 3), linear())}
                    extras.update({7 + 3 * t: (lambda t=t: (deep_bias(1, t), deep_root(HID_T + t))) for t in range(HID_T)})
                high_parts(first_of_l2(j), bt, 2, extras)
                if j == BLOCKS - 1:
                    for t in range(HID_T):
                        deep_act(1, t)
                out_of_l2(first_of_l2(j) + L2_TILES, j, bt)

            steps(sc, step)
            sc.wait_ge(s_acc, 1)
            nc.scalar.activation(res[:, :], p_t[1][0:1, :], ACT.Identity, bias=ob_sb[:, :]).then_inc(s_res, 1)


def kernel(**inputs):
    import numpy as _np
    import concourse.bacc as _bacc
    from concourse import mybir as _mybir
    from concourse.bass_utils import run_bass_kernel_spmd as _run

    a = {k.replace("L0_rec_", ""): _np.asarray(v) for k, v in inputs.items()}
    w1 = a["conv_w1"]
    i = _np.arange(FIELDS)
    order = [k for tile in OFFSETS for k in tile]
    fwd = _np.concatenate([w1[:, i, (i + k) % FIELDS].T for k in order] + [w1[:, i, i].T])
    bwd = _np.concatenate([w1[:, (i + k) % FIELDS, i].T for k in order] + [w1[:, i, i].T])

    def tiles(w):
        return w.reshape(L1_TILES, 3 * FIELDS, H1).transpose(1, 0, 2)

    def hidden(v):
        return v.reshape(HID_T, HID_K).T

    ow = a["out_w"]
    cuts = [0, 1, 1 + NEXT, 1 + NEXT + H2, 1 + NEXT + H2 + HIDDEN]
    ow_lin, ow_hi, ow_h2, ow_y = (ow[cuts[n]:cuts[n + 1]] for n in range(4))
    sent = {
        "idx": a["r_feat_index"], "emb": a["emb_table"],
        "lin_w": a["linear_w"].reshape(FLAT_T, FLAT_K).T, "lin_b": a["linear_b"].reshape(1, 1),
        "w1a": tiles(fwd), "w1b": tiles(bwd), "b1": a["conv_b1"].reshape(H1, 1),
        "w2": a["conv_w2"].transpose(2, 1, 0).reshape(FIELDS * NEXT, H2), "b2": a["conv_b2"].reshape(H2, 1),
        "dw1": a["deep_w1"], "db1": hidden(a["deep_b1"]), "g1": hidden(a["bn_g1"]), "be1": hidden(a["bn_b1"]),
        "dw2": a["deep_w2"], "db2": hidden(a["deep_b2"]), "g2": hidden(a["bn_g2"]), "be2": hidden(a["bn_b2"]),
        "ow_lin": ow_lin, "ow_hi": ow_hi, "ow_h2": ow_h2, "ow_y": hidden(ow_y), "ob": a["out_b"].reshape(1, 1),
    }
    nc = _bacc.Bacc("TRN2", target_bir_lowering=False, num_devices=1)
    arrays, args = {}, []
    for name, v in sent.items():
        v = _np.ascontiguousarray(v)
        arrays[f"in_{name}"] = v
        args.append(nc.dram_tensor(f"in_{name}", v.shape, _mybir.dt.from_np(v.dtype), kind="ExternalInput").ap())
    out = nc.dram_tensor("out_y", (BATCH, 1), _mybir.dt.float32, kind="ExternalOutput").ap()
    build(nc, *args, out)
    r = _run(nc, [arrays], core_ids=[0])
    return r.results[0]["out_y"]
```

```python
import concourse.bass as bass
from concourse import mybir
from contextlib import ExitStack


BATCH, FIELDS, DIM, VOCAB = 512, 39, 16, 125000
H1, H2 = 128, 128
NEXT = H1 // 2
HIDDEN = 400
FLAT = FIELDS * DIM
BN_EPS = 1e-5

ROWS = 128
TILES = BATCH // ROWS
TOK = 1024
HALF_D = TOK // ROWS
BLOCKS = BATCH * DIM // TOK
BANK = 512
CHUNKS = TOK // BANK

OFFSETS = [[3 * t + 1, 3 * t + 2, 3 * t + 3] for t in range(6)] + [[19, 0]]
L1_TILES = len(OFFSETS)
L2_PAIRS = FIELDS // 2
TAIL = L2_PAIRS
L2_ORDER = [TAIL] + list(range(L2_PAIRS))
L2_TILES = len(L2_ORDER)
PER_STEP = L1_TILES + L2_TILES
RING = 9
SPLIT_RING = 4

L1_SPLIT = [1, 3, 5]
L2_SPLIT = [TAIL, 1, 3, 5, 7, 9, 11, 13, 15]
SPLITS_PER_STEP = len(L1_SPLIT) + len(L2_SPLIT)
assert PER_STEP % RING == 0 and SPLITS_PER_STEP % SPLIT_RING == 0

L1_SEQ = [(1, t) for t in range(L1_TILES)]
L2_SEQ = [(2, t) for t in L2_ORDER]
SEQ = L1_SEQ + (L1_SEQ + L2_SEQ) * (BLOCKS - 1) + L2_SEQ

FLAT_K = 104
FLAT_T = FLAT // FLAT_K
HID_K = 100
HID_T = HIDDEN // HID_K


def is_split(tile):
    layer, t = tile
    return t in (L1_SPLIT if layer == 1 else L2_SPLIT)


def loads_of(tile):
    layer, t = tile
    return len(OFFSETS[t]) if layer == 1 else 2


def rows_of(tile):
    layer, t = tile
    return FIELDS * len(OFFSETS[t]) if layer == 1 else 128


def splits_before(s):
    return sum(is_split(x) for x in SEQ[:s])


def seq_of_split(q):
    return [s for s, x in enumerate(SEQ) if is_split(x)][q]


def loads_landed(s):
    return 16 * sum(loads_of(SEQ[r]) for r in range(s % RING, s + 1, RING))


def first_of_l1(j):
    return 0 if j == 0 else L1_TILES + PER_STEP * (j - 1)


def first_of_l2(j):
    return first_of_l1(j + 1) + (L1_TILES if j < BLOCKS - 1 else 0)


def build(nc, idx, emb, lin_w, lin_b, w1a, w1b, b1, w2, b2, dw1, db1, g1, be1, dw2, db2, g2, be2,
          ow_lin, ow_hi, ow_h2, ow_y, ob, out):
    F32, F32R, I32 = mybir.dt.float32, mybir.dt.float32r, mybir.dt.int32
    ALU, ACT, AX = mybir.AluOpType, mybir.ActivationFunctionType, mybir.AxisListType

    xs = nc.dram_tensor("xs_scratch", [2 * FIELDS, BATCH * DIM], F32).ap()

    ctx = ExitStack()
    with ctx:
        def sb(name, shape, dt=F32):
            return ctx.enter_context(nc.sbuf_tensor(name, shape, dt))

        def ps(name, shape, dt=F32):
            return ctx.enter_context(nc.psum_tensor(name, shape, dt))

        def sem(name):
            return ctx.enter_context(nc.semaphore(name))

        idx_raw = sb("idx_raw", [ROWS, TILES, FIELDS], I32)
        idx_wrap = sb("idx_wrap", [ROWS, TILES, FIELDS], F32)
        idx_all = sb("idx_all", [ROWS, TILES, FIELDS], I32)
        idx_cur = sb("idx_cur", [ROWS, FIELDS], I32)
        G = sb("G", [ROWS, FLAT])
        ident = sb("ident", [128, 128])
        xT = sb("xT", [FIELDS, DIM * ROWS])
        flatT = sb("flatT", [FLAT_K, FLAT_T, BATCH])
        ring = sb("ring", [128, RING, TOK])
        zh = sb("zh", [128, SPLIT_RING, TOK], F32R)
        zl = sb("zl", [128, SPLIT_RING, TOK], F32R)
        xa = sb("xa", [3 * FIELDS, 2, TOK])
        nx = sb("nx", [128, 2, TOK])
        hi = sb("hi", [128, TOK])
        h2s = sb("h2s", [128, TOK])
        hi_sum = sb("hi_sum", [128, 2, TILES, ROWS])
        h2_sum = sb("h2_sum", [128, 2, TILES, ROWS])
        w1s = sb("w1s", [3 * FIELDS, L1_TILES, H1])
        w1b_sb = sb("w1b_sb", [3 * FIELDS, L1_TILES, H1])
        w2s = sb("w2s", [128, L2_TILES, H2])
        w1h = sb("w1h", [3 * FIELDS, len(L1_SPLIT), H1], F32R)
        w1l = sb("w1l", [3 * FIELDS, len(L1_SPLIT), H1], F32R)
        w2h = sb("w2h", [128, len(L2_SPLIT), H2], F32R)
        w2l = sb("w2l", [128, len(L2_SPLIT), H2], F32R)
        b1_sb = sb("b1_sb", [H1, 1])
        b1_dup = sb("b1_dup", [128, 1])
        b2_sb = sb("b2_sb", [H2, 1])
        dw1_sb = sb("dw1_sb", [FLAT_K, FLAT_T, HIDDEN])
        dw2_sb = sb("dw2_sb", [HID_K, HID_T, HIDDEN])
        vec = sb("vec", [HID_K, 6, HID_T])
        lw_sb = sb("lw_sb", [FLAT_K, FLAT_T])
        lb_sb = sb("lb_sb", [1, 1])
        pre = sb("pre", [HID_K, HID_T, BATCH])
        act = sb("act", [HID_K, HID_T, BATCH])
        stats = sb("stats", [HID_K, HID_T, 6])
        mv = sb("mv", [HID_K, HID_T, 2])
        bn = sb("bn", [HID_K, 8, HID_T])
        scale = sb("scale", [HID_K, 2, HID_T])
        shift = sb("shift", [HID_K, 2, HID_T])
        ow_lin_sb = sb("ow_lin_sb", [1, 1])
        ow_hi_sb = sb("ow_hi_sb", [128, 1])
        ow_h2_sb = sb("ow_h2_sb", [H2, 1])
        ow_y_sb = sb("ow_y_sb", [HID_K, HID_T])
        ob_sb = sb("ob_sb", [1, 1])
        lin = sb("lin", [1, BATCH])
        res = sb("res", [1, BATCH])

        p_h1 = ps("p_h1", [H1, TOK])
        p_h2 = ps("p_h2", [H2, TOK])
        p_t = [ps(f"p_t{i}", [128, BANK]) for i in range(2)]
        p_d = [ps(f"p_d{i}", [128, BANK]) for i in range(2)]

        s_idx = sem("s_idx")
        s_clamp = sem("s_clamp")
        s_w = sem("s_w")
        s_small = sem("s_small")
        s_ident = sem("s_ident")
        s_cur = sem("s_cur")
        s_gather = sem("s_gather")
        s_sym = sem("s_sym")
        s_wh = sem("s_wh")
        s_wl = sem("s_wl")
        s_tp = sem("s_tp")
        s_te = sem("s_te")
        s_xs = [sem(f"s_xs{c}") for c in range(2)]
        s_load = [sem(f"s_load{r}") for r in range(RING)]
        s_xa = [sem(f"s_xa{p}") for p in range(2)]
        s_xa_free = sem("s_xa_free")
        s_z = sem("s_z")
        s_zh = sem("s_zh")
        s_zl = sem("s_zl")
        s_used = sem("s_used")
        s_n = sem("s_n")
        s_n_free = sem("s_n_free")
        s_hi = sem("s_hi")
        s_hi_sum = sem("s_hi_sum")
        s_h2 = sem("s_h2")
        s_h2_sum = sem("s_h2_sum")
        s_dp = sem("s_dp")
        s_pre = sem("s_pre")
        s_bn = sem("s_bn")
        s_eps = sem("s_eps")
        s_root = sem("s_root")
        s_coef = sem("s_coef")
        s_act = sem("s_act")
        s_lin_p = sem("s_lin_p")
        s_lin = sem("s_lin")
        s_acc = sem("s_acc")
        s_res = sem("s_res")
        s_out = sem("s_out")

        s_past = sem("s_past")

        def own_wait(eng, semaphore, value):
            eng.wait_ge(semaphore, value)
            eng.sem_inc(s_past, 1)

        block = ctx.enter_context(nc.Block())

        TP_GROUPS = DIM // 4 + FLAT_T // 3
        T_AT = {2: (0, 1), 6: (2, 3), 10: (4, 5)}
        LAG = 6
        DEEP1_AT = (0, 3, 6, 9)
        DEEP2_AT = (7, 9, 11, 13)
        H1_OUT, H1_SUM = 5, 13
        H2_OUT, H2_SUM = 5, 3

        def steps(eng, step):
            step(0, 0)
            with eng.Fori(0, 2) as bt:
                step(1, bt)
                step(2, bt)
            for j in range(5, BLOCKS):
                step(j, 0)

        @block.sync
        def _(sp):
            sp.dma_start(idx_raw[:, :, :], idx.rearrange("(t p) f -> p t f", p=ROWS)).then_inc(s_idx, 16)
            sp.dma_start(w1s[:, 0:6, :], w1a[:, 0:6, :]).then_inc(s_w, 16)
            sp.dma_start(w1s[0:78, 6, :], w1a[0:78, 6, :]).then_inc(s_w, 16)
            sp.dma_start(w1b_sb[:, 0:6, :], w1b[:, 0:6, :]).then_inc(s_w, 16)
            sp.dma_start(w1b_sb[0:39, 6, :], w1b[0:39, 6, :]).then_inc(s_w, 16)
            sp.dma_start(w2s[:, 0:L2_PAIRS, :], w2[0:128 * L2_PAIRS, :].rearrange("(t p) o -> p t o", p=128)).then_inc(s_w, 16)
            for half in range(2):
                sp.dma_start(w2s[NEXT * half:NEXT * (half + 1), TAIL, :], w2[128 * L2_PAIRS:, :]).then_inc(s_w, 16)
            sp.dma_start(b1_sb[:, :], b1).then_inc(s_small, 16)
            for half in range(2):
                sp.dma_start(b1_dup[NEXT * half:NEXT * (half + 1), :], b1[0:NEXT, :]).then_inc(s_small, 16)
            sp.dma_start(b2_sb[:, :], b2).then_inc(s_small, 16)
            sp.dma_start(dw1_sb[:, :, :], dw1.rearrange("(t p) o -> p t o", p=FLAT_K)).then_inc(s_small, 16)
            sp.dma_start(dw2_sb[:, :, :], dw2.rearrange("(t p) o -> p t o", p=HID_K)).then_inc(s_small, 16)
            for n, v in enumerate((db1, g1, be1, db2, g2, be2)):
                sp.dma_start(vec[:, n, :], v).then_inc(s_small, 16)
            for dst, src in ((lw_sb, lin_w), (lb_sb, lin_b), (ow_lin_sb, ow_lin), (ow_h2_sb, ow_h2),
                             (ow_y_sb, ow_y), (ob_sb, ob)):
                sp.dma_start(dst[:, :], src).then_inc(s_small, 16)
            sp.dma_start(ow_hi_sb[NEXT:128, :], ow_hi).then_inc(s_small, 16)

            def load_tiles(seq0, j, bt, layer, k):
                col = (j + 2 * bt) * TOK
                if layer == 1:
                    own_wait(sp, s_xs[j % 2], 32 * (j // 2 + 1) + 32 * bt)
                    own_wait(sp, s_xa_free, j + 1 + 2 * bt)
                    for q in range(3):
                        sp.dma_start(xa[FIELDS * q:FIELDS * (q + 1), j % 2, :],
                                     xs[0:FIELDS, bass.ds(col, TOK)]).then_inc(s_xa[j % 2], 16)
                for n, (_, t) in enumerate(L1_SEQ if layer == 1 else L2_SEQ):
                    s = seq0 + n
                    slot = s % RING
                    own_wait(sp, s_used, s + 1 + 2 * PER_STEP * bt)
                    if layer == 1:
                        for q, off in enumerate(OFFSETS[t]):
                            sp.dma_start(ring[FIELDS * q:FIELDS * (q + 1), slot, :],
                                         xs[off:off + FIELDS, bass.ds(col, TOK)]).then_inc(s_load[slot], 16)
                    else:
                        for half in range(2):
                            m = min(2 * t + half, FIELDS - 1)
                            sp.dma_start(ring[NEXT * half:NEXT * (half + 1), slot, :],
                                         xs[m:m + 1, bass.ds(col, TOK)].broadcast_to([NEXT, TOK])).then_inc(s_load[slot], 16)

            load_tiles(0, 0, 0, 1, 0)

            def step(j, bt):
                if j + 1 < BLOCKS:
                    load_tiles(first_of_l1(j + 1), j + 1, bt, 1, 0)
                load_tiles(first_of_l2(j), j, bt, 2, 0)

            steps(sp, step)

            sp.wait_ge(s_res, 1)
            sp.dma_start(out.rearrange("b o -> o b"), res[:, :]).then_inc(s_out, 16)
            sp.wait_ge(s_out, 16)

        @block.gpsimd
        def _(pool):
            def gather():
                for f in range(FIELDS):
                    nc.gpsimd.indirect_dma_start(
                        G[:, DIM * f:DIM * (f + 1)], None, emb[:, :],
                        bass.IndirectOffsetOnAxis(idx_cur[:, f:f + 1], 0)).then_inc(s_gather, 16)

            pool.wait_ge(s_clamp, 3)
            nc.gpsimd.tensor_copy(idx_cur[:, :], idx_all[:, 0, :]).then_inc(s_cur, 1)
            pool.wait_ge(s_cur, 1)
            gather()
            nc.gpsimd.memset(ident[:, :], 0.0).then_inc(s_ident, 1)
            pool.wait_ge(s_ident, 1)
            nc.gpsimd.affine_select(out=ident[:, :], in_=ident[:, :], compare_op=ALU.not_equal, fill=1.0,
                                    base=0, pattern=[[-1, 128]], channel_multiplier=1).then_inc(s_ident, 1)
            with pool.Fori(1, TILES) as t:
                own_wait(pool, s_tp, TP_GROUPS * t)
                nc.gpsimd.tensor_copy(idx_cur[:, :], idx_all[:, bass.ds(t, 1), :].rearrange("p a f -> p (a f)")).then_inc(s_cur, 1)
                own_wait(pool, s_cur, t + 1)
                gather()

        @block.vector
        def _(dve):
            nc.vector.sem_inc(s_xa_free, 2)
            dve.wait_ge(s_idx, 16)
            nc.vector.tensor_scalar(idx_wrap[:, :, :], idx_raw[:, :, :], 0.0, float(VOCAB), ALU.is_lt, ALU.mult).then_inc(s_clamp, 1)
            dve.wait_ge(s_clamp, 1)
            nc.vector.tensor_tensor(idx_wrap[:, :, :], idx_wrap[:, :, :], idx_raw[:, :, :], ALU.add).then_inc(s_clamp, 1)
            dve.wait_ge(s_clamp, 2)
            nc.vector.tensor_scalar(idx_all[:, :, :], idx_wrap[:, :, :], 0.0, float(VOCAB - 1), ALU.max, ALU.min).then_inc(s_clamp, 1)

            dve.wait_ge(s_w, 7 * 16)
            nc.vector.tensor_tensor(w1s[:, 0:6, :], w1s[:, 0:6, :], w1b_sb[:, 0:6, :], ALU.add).then_inc(s_sym, 1)
            nc.vector.tensor_tensor(w1s[0:39, 6, :], w1s[0:39, 6, :], w1b_sb[0:39, 6, :], ALU.add).then_inc(s_sym, 1)
            dve.wait_ge(s_wh, 1)
            dve.wait_ge(s_sym, 2)
            for n, t in enumerate(L1_SPLIT):
                nc.vector.tensor_tensor(w1l[:, n, :], w1s[:, t, :], w1h[:, n, :].bitcast(F32), ALU.subtract)
            for n, t in enumerate(L2_SPLIT):
                last = nc.vector.tensor_tensor(w2l[:, n, :], w2s[:, t, :], w2h[:, n, :].bitcast(F32), ALU.subtract)
            last.then_inc(s_wl, 1)

            def low_part(s, bt):
                q = splits_before(s)
                dve.wait_ge(s_zh, q + 1 + 2 * SPLITS_PER_STEP * bt)
                if q >= SPLIT_RING:
                    dve.wait_ge(s_used, RING + seq_of_split(q - SPLIT_RING) + 1 + 2 * PER_STEP * bt)
                slot, part, r = s % RING, q % SPLIT_RING, rows_of(SEQ[s])
                if SEQ[s] == (2, TAIL):
                    nc.vector.tensor_tensor(zh[NEXT:128, part, :], ring[NEXT:128, slot, :],
                                            zh[NEXT:128, part, :].bitcast(F32), ALU.subtract).then_inc(s_zl, 1)
                else:
                    nc.vector.tensor_tensor(zl[0:r, part, :], ring[0:r, slot, :],
                                            zh[0:r, part, :].bitcast(F32), ALU.subtract).then_inc(s_zl, 1)

            def products(seq0, j, bt, layer, extras):
                if layer == 1:
                    dve.wait_ge(s_xa[j % 2], 48 * (j // 2 + 1) + 48 * bt)
                else:
                    dve.wait_ge(s_n, j + 1 + 2 * bt)
                tiles = L1_SEQ if layer == 1 else L2_SEQ
                for n, tile in enumerate(tiles):
                    s = seq0 + n
                    slot, r = s % RING, rows_of(tile)
                    per = (loads_landed(s + 2 * PER_STEP) if s + 2 * PER_STEP < len(SEQ) else 0) - loads_landed(s)
                    dve.wait_ge(s_load[slot], loads_landed(s) + (per * bt if per > 0 else 0))
                    by = xa[0:r, j % 2, :] if layer == 1 else nx[:, j % 2, :]
                    last = nc.vector.tensor_tensor(ring[0:r, slot, :], by, ring[0:r, slot, :], ALU.mult).then_inc(s_z, 1)
                    if n and is_split(tiles[n - 1]):
                        low_part(s - 1, bt)
                    for work in [w for at, w in extras if at == n]:
                        work()
                dve.wait_ge(s_z, seq0 + len(tiles) + 2 * PER_STEP * bt)
                nc.vector.sem_inc(s_xa_free if layer == 1 else s_n_free, 1)

            def sum_d(dst, src, j, bt):
                return nc.vector.tensor_reduce(
                    dst[:, j % 2, bass.ds(j // 2 + bt, 1), :].rearrange("p a b -> p (a b)"),
                    src.rearrange("p (d b) -> p b d", d=HALF_D), AX.X, ALU.add)

            def sum_h2(j, bt):
                dve.wait_ge(s_h2, j + 1 + 2 * bt)
                sum_d(h2_sum[:, :, :, :], h2s[:, :], j, bt).then_inc(s_h2_sum, 1)

            def sum_hi(j, bt):
                dve.wait_ge(s_hi, j + 1 + 2 * bt)
                sum_d(hi_sum[NEXT:128, :, :, :], hi[NEXT:128, :], j, bt).then_inc(s_hi_sum, 1)

            count = [0]

            def chain(ins):
                count[0] += 1
                ins.then_inc(s_bn, 1)
                dve.wait_ge(s_bn, count[0])

            def statistics(layer, t):
                dve.wait_ge(s_pre, layer * HID_T + t + 1)
                chain(nc.vector.bn_stats(stats[:, t, :], pre[:, t, :]))
                chain(nc.vector.bn_aggr(mv[:, t, :], stats[:, t, :]))

            def add_eps(layer):
                nc.vector.tensor_scalar(bn[:, 0, :], mv[:, :, 1], BN_EPS, None, ALU.add).then_inc(s_eps, 1)

            def coefficients(layer):
                dve.wait_ge(s_root, layer + 1)
                chain(nc.vector.reciprocal(bn[:, 2, :], bn[:, 1, :]))
                chain(nc.vector.tensor_tensor(bn[:, 3, :], bn[:, 0, :], bn[:, 2, :], ALU.mult))
                chain(nc.vector.tensor_tensor(bn[:, 4, :], bn[:, 3, :], bn[:, 1, :], ALU.add))
                chain(nc.vector.tensor_scalar(bn[:, 5, :], bn[:, 4, :], 0.5, None, ALU.mult))
                chain(nc.vector.reciprocal(bn[:, 6, :], bn[:, 5, :]))
                chain(nc.vector.tensor_tensor(scale[:, layer, :], bn[:, 6, :], vec[:, 3 * layer + 1, :], ALU.mult))
                chain(nc.vector.tensor_tensor(bn[:, 7, :], mv[:, :, 0], scale[:, layer, :], ALU.mult))
                nc.vector.tensor_tensor(shift[:, layer, :], vec[:, 3 * layer + 2, :], bn[:, 7, :], ALU.subtract).then_inc(s_coef, 1)

            products(0, 0, 0, 1, [])

            def step(j, bt):
                if j + 1 < BLOCKS:
                    products(first_of_l1(j + 1), j + 1, bt, 1, [] if j else [(4, lambda: sum_hi(0, 0))])
                extras = []
                if j:
                    extras += [(H2_SUM, lambda: sum_h2(j - 1, bt))]
                if j + 1 < BLOCKS:
                    extras += [(H1_SUM, lambda: sum_hi(j + 1, bt))]
                if j == BLOCKS - 2:
                    extras += [(n + LAG + 1, lambda t=t: statistics(0, t)) for t, n in enumerate(DEEP1_AT)]
                    extras += [(17, lambda: add_eps(0))]
                    extras += [(18, lambda: (dve.wait_ge(s_small, 19 * 16), coefficients(0)))]
                if j == BLOCKS - 1:
                    extras = [(6, lambda: sum_h2(j - 1, bt))]
                    extras += [(n + LAG, lambda t=t: statistics(1, t)) for t, n in enumerate(DEEP2_AT[:-1])]
                products(first_of_l2(j), j, bt, 2, extras)

            steps(dve, step)
            statistics(1, HID_T - 1)
            add_eps(1)
            coefficients(1)
            sum_h2(BLOCKS - 1, 0)

        @block.tensor
        def _(pe):
            nc.tensor.sem_inc(s_used, RING)

            def transposes(t, bt, groups=range(TP_GROUPS)):
                if groups[0] == 0:
                    own_wait(pe, s_gather, 16 * FIELDS * (t + 1) + 16 * FIELDS * bt)
                by_d = G[:, :].rearrange("p (f d) -> p d f", d=DIM)
                for g in groups:
                    n = TP_GROUPS * t + g
                    if n >= 2:
                        own_wait(pe, s_te, n - 1 + TP_GROUPS * bt)
                    bank = p_t[g % 2]
                    if g < DIM // 4:
                        for c in range(4):
                            last = nc.tensor.transpose(bank[0:FIELDS, 128 * c:128 * (c + 1)], by_d[:, 4 * g + c, :], ident[:, :])
                    else:
                        for c in range(3):
                            k = 3 * (g - DIM // 4) + c
                            last = nc.tensor.transpose(bank[0:FLAT_K, 128 * c:128 * (c + 1)],
                                                       G[:, FLAT_K * k:FLAT_K * (k + 1)], ident[:, :])
                    last.then_inc(s_tp, 1)

            def contract(seq0, j, bt, layer, extras):
                acc = p_h1 if layer == 1 else p_h2
                tiles = L1_SEQ if layer == 1 else L2_SEQ
                if layer == 1 and j:
                    pe.wait_ge(s_hi, j + 2 * bt)
                if layer == 2 and j:
                    pe.wait_ge(s_h2, j + 2 * bt)
                for n, tile in enumerate(tiles):
                    s = seq0 + n
                    t, slot, r = tile[1], s % RING, rows_of(tile)
                    first, final = n == 0, n == len(tiles) - 1

                    def mm(c, w, x, start=False, stop=False):
                        return nc.tensor.matmul(acc[:, BANK * c:BANK * (c + 1)], w, x[:, BANK * c:BANK * (c + 1)],
                                                start=start, stop=stop)

                    if not is_split(tile):
                        pe.wait_ge(s_z, s + 1 + 2 * PER_STEP * bt)
                        w = (w1s if layer == 1 else w2s)[0:r, t, :]
                        for c in range(CHUNKS):
                            last = mm(c, w, ring[0:r, slot, :], first, final)
                    else:
                        q = splits_before(s)
                        part = q % SPLIT_RING
                        k = (L1_SPLIT if layer == 1 else L2_SPLIT).index(t)
                        wh, wl = ((w1h, w1l) if layer == 1 else (w2h, w2l))
                        wh, wl = wh[0:r, k, :], wl[0:r, k, :]
                        high, low = zh[0:r, part, :], zl[0:r, part, :]
                        if t == TAIL and layer == 2:
                            pe.wait_ge(s_zl, q + 1 + 2 * SPLITS_PER_STEP * bt)
                            for c in range(CHUNKS):
                                mm(c, wl, high, first)
                            for c in range(CHUNKS):
                                last = mm(c, wh, high, False, final)
                        else:
                            pe.wait_ge(s_zh, q + 1 + 2 * SPLITS_PER_STEP * bt)
                            for c in range(CHUNKS):
                                mm(c, wl, high, first)
                            for c in range(CHUNKS):
                                mm(c, wh, high)
                            pe.wait_ge(s_zl, q + 1 + 2 * SPLITS_PER_STEP * bt)
                            for c in range(CHUNKS):
                                last = mm(c, wh, low, False, final)
                    last.then_inc(s_used, 1)
                    for work in [w for at, w in extras if at == n]:
                        work()

            def deep(layer, t):
                n = layer * HID_T + t
                if n >= 2:
                    pe.wait_ge(s_pre, n - 1)
                if layer == 0:
                    if t == 0:
                        pe.wait_ge(s_te, TP_GROUPS * TILES)
                        pe.wait_ge(s_small, 19 * 16)
                    src, w, k = flatT, dw1_sb, FLAT_T
                else:
                    if t == 0:
                        pe.wait_ge(s_act, HID_T)
                    src, w, k = act, dw2_sb, HID_T
                for c in range(k):
                    last = nc.tensor.matmul(p_d[n % 2][0:HID_K, :], w[:, c, HID_K * t:HID_K * (t + 1)], src[:, c, :],
                                            start=c == 0, stop=c == k - 1)
                last.then_inc(s_dp, 1)

            def linear():
                for c in range(FLAT_T):
                    last = nc.tensor.matmul(p_t[0][0:1, :], lw_sb[:, c:c + 1], flatT[:, c, :], start=c == 0, stop=c == FLAT_T - 1)
                last.then_inc(s_lin_p, 1)

            pe.wait_ge(s_ident, 2)
            transposes(0, 0)
            pe.wait_ge(s_wl, 1)
            contract(0, 0, 0, 1, [])

            def step(j, bt):
                if j + 1 < BLOCKS:
                    contract(first_of_l1(j + 1), j + 1, bt, 1, [])
                extras = []
                if j % 2 == 0 and j < BLOCKS - 2:
                    extras += [(n, lambda g=g: transposes(j // 2 + 1, bt, g)) for n, g in T_AT.items()]
                if j == BLOCKS - 2:
                    extras += [(n, lambda t=t: deep(0, t)) for t, n in enumerate(DEEP1_AT)]
                if j == BLOCKS - 1:
                    extras += [(n, lambda t=t: deep(1, t)) for t, n in enumerate(DEEP2_AT)]
                    extras += [(2, linear)]
                contract(first_of_l2(j), j, bt, 2, extras)

            steps(pe, step)

            total = p_t[1][0:1, :]
            pe.wait_ge(s_lin, 1)
            nc.tensor.matmul(total, ow_lin_sb[:, :], lin[:, :], start=True, stop=False)
            pe.wait_ge(s_hi_sum, BLOCKS)
            for c in range(2):
                nc.tensor.matmul(total, ow_hi_sb[NEXT:128, :], hi_sum[NEXT:128, c, :, :].rearrange("p t b -> p (t b)"), start=False, stop=False)
            pe.wait_ge(s_act, 2 * HID_T)
            for t in range(HID_T):
                nc.tensor.matmul(total, ow_y_sb[:, t:t + 1], act[:, t, :], start=False, stop=False)
            pe.wait_ge(s_h2_sum, BLOCKS)
            for c in range(2):
                last = nc.tensor.matmul(total, ow_h2_sb[:, :], h2_sum[:, c, :, :].rearrange("p t b -> p (t b)"), start=False, stop=c == 1)
            last.then_inc(s_acc, 1)

        @block.scalar
        def _(sc):
            nc.scalar.sem_inc(s_n_free, 2)

            sc.wait_ge(s_sym, 2)
            for n, t in enumerate(L1_SPLIT):
                nc.scalar.activation(w1h[:, n, :], w1s[:, t, :], ACT.Copy)
            for n, t in enumerate(L2_SPLIT):
                last = nc.scalar.activation(w2h[:, n, :], w2s[:, t, :], ACT.Copy)
            last.then_inc(s_wh, 1)

            def out_of_transposes(t, bt, groups=range(TP_GROUPS)):
                for g in groups:
                    n = TP_GROUPS * t + g
                    sc.wait_ge(s_tp, n + 1 + TP_GROUPS * bt)
                    if g < DIM // 4:
                        if t and g % 2 == 0:
                            sc.wait_ge(s_xs[g // 2], 32 * t + 32 * bt)
                        nc.scalar.activation(xT[:, BANK * g:BANK * (g + 1)], p_t[g % 2][0:FIELDS, :], ACT.Copy).then_inc(s_te, 1)
                        if g % 2:
                            half = g // 2
                            sc.wait_ge(s_te, n + 1 + TP_GROUPS * bt)
                            for copy in range(2):
                                sc.dma_start(xs[FIELDS * copy:FIELDS * (copy + 1), bass.ds((2 * t + half) * TOK + 2 * TOK * bt, TOK)],
                                             xT[:, TOK * half:TOK * (half + 1)]).then_inc(s_xs[half], 16)
                    else:
                        k = 3 * (g - DIM // 4)
                        nc.scalar.activation(
                            flatT[:, k:k + 3, bass.ds(ROWS * t + ROWS * bt, ROWS)],
                            p_t[g % 2][0:FLAT_K, 0:3 * ROWS].rearrange("p (k b) -> p k b", k=3), ACT.Copy).then_inc(s_te, 1)

            def high_parts(seq0, bt, layer, extras):
                tiles = L1_SEQ if layer == 1 else L2_SEQ
                for n, tile in enumerate(tiles):
                    s = seq0 + n
                    if is_split(tile):
                        q = splits_before(s)
                        sc.wait_ge(s_z, s + 1 + 2 * PER_STEP * bt)
                        if q >= SPLIT_RING:
                            sc.wait_ge(s_used, RING + seq_of_split(q - SPLIT_RING) + 1 + 2 * PER_STEP * bt)
                        r = rows_of(tile)
                        nc.scalar.activation(zh[0:r, q % SPLIT_RING, :], ring[0:r, s % RING, :], ACT.Copy).then_inc(s_zh, 1)
                    for work in [w for at, w in extras if at == n]:
                        work()

            def out_of_l1(seq_end, j, bt):
                sc.wait_ge(s_used, RING + seq_end + 2 * PER_STEP * bt)
                sc.wait_ge(s_n_free, j + 1 + 2 * bt)
                nc.scalar.activation(nx[0:NEXT, j % 2, :], p_h1[0:NEXT, :], ACT.Relu, bias=b1_dup[0:NEXT, :])
                nc.scalar.activation(nx[NEXT:128, j % 2, :], p_h1[0:NEXT, :], ACT.Relu, bias=b1_dup[NEXT:128, :]).then_inc(s_n, 1)
                if j:
                    sc.wait_ge(s_hi_sum, j + 2 * bt)
                nc.scalar.activation(hi[NEXT:128, :], p_h1[NEXT:128, :], ACT.Relu, bias=b1_sb[NEXT:128, :]).then_inc(s_hi, 1)

            def out_of_l2(seq_end, j, bt):
                sc.wait_ge(s_used, RING + seq_end + 2 * PER_STEP * bt)
                if j:
                    sc.wait_ge(s_h2_sum, j + 2 * bt)
                nc.scalar.activation(h2s[:, :], p_h2[:, :], ACT.Relu, bias=b2_sb[:, :]).then_inc(s_h2, 1)

            def deep_bias(layer, t):
                n = layer * HID_T + t
                sc.wait_ge(s_dp, n + 1)
                if layer:
                    sc.wait_ge(s_act, HID_T)
                nc.scalar.activation(pre[:, t, :], p_d[n % 2][0:HID_K, :], ACT.Identity, bias=vec[:, 3 * layer, t:t + 1]).then_inc(s_pre, 1)

            def deep_root(layer):
                sc.wait_ge(s_eps, layer + 1)
                nc.scalar.activation(bn[:, 1, :], bn[:, 0, :], ACT.Sqrt).then_inc(s_root, 1)

            def deep_act(layer):
                sc.wait_ge(s_coef, layer + 1)
                if layer:
                    sc.wait_ge(s_dp, 2 * HID_T)
                for t in range(HID_T):
                    nc.scalar.activation(act[:, t, :], pre[:, t, :], ACT.Relu, bias=shift[:, layer, t:t + 1],
                                         scale=scale[:, layer, t:t + 1]).then_inc(s_act, 1)

            def linear():
                sc.wait_ge(s_lin_p, 1)
                nc.scalar.activation(lin[:, :], p_t[0][0:1, :], ACT.Identity, bias=lb_sb[:, :]).then_inc(s_lin, 1)

            out_of_transposes(0, 0)
            high_parts(0, 0, 1, [])
            sc.wait_ge(s_small, 19 * 16)
            out_of_l1(L1_TILES, 0, 0)

            def step(j, bt):
                before = [(H2_OUT, lambda: out_of_l2(first_of_l2(j - 1) + L2_TILES, j - 1, bt))] if j else []
                extras = []
                if j + 1 < BLOCKS:
                    high_parts(first_of_l1(j + 1), bt, 1, before)
                    extras += [(H1_OUT, lambda: out_of_l1(first_of_l1(j + 1) + L1_TILES, j + 1, bt))]
                else:
                    extras += before
                if j % 2 == 0 and j < BLOCKS - 2:
                    extras += [(n + LAG, lambda g=g: out_of_transposes(j // 2 + 1, bt, g)) for n, g in T_AT.items()]
                if j == BLOCKS - 2:
                    extras += [(n + LAG, lambda t=t: deep_bias(0, t)) for t, n in enumerate(DEEP1_AT)]
                    extras += [(17, lambda: deep_root(0))]
                    extras += [(18, lambda: deep_act(0))]
                if j == BLOCKS - 1:
                    extras += [(n + LAG, lambda t=t: deep_bias(1, t)) for t, n in enumerate(DEEP2_AT)]
                    extras += [(8, linear)]
                high_parts(first_of_l2(j), bt, 2, extras)
                if j == BLOCKS - 1:
                    deep_root(1)
                    deep_act(1)
                    out_of_l2(first_of_l2(j) + L2_TILES, j, bt)

            steps(sc, step)
            sc.wait_ge(s_acc, 1)
            nc.scalar.activation(res[:, :], p_t[1][0:1, :], ACT.Identity, bias=ob_sb[:, :]).then_inc(s_res, 1)


def kernel(**inputs):
    import numpy as _np
    import concourse.bacc as _bacc
    from concourse import mybir as _mybir
    from concourse.bass_utils import run_bass_kernel_spmd as _run

    a = {k.replace("L0_rec_", ""): _np.asarray(v) for k, v in inputs.items()}
    w1 = a["conv_w1"]
    i = _np.arange(FIELDS)
    order = [k for tile in OFFSETS for k in tile]
    fwd = _np.concatenate([w1[:, i, (i + k) % FIELDS].T for k in order] + [w1[:, i, i].T])
    bwd = _np.concatenate([w1[:, (i + k) % FIELDS, i].T for k in order] + [w1[:, i, i].T])

    def tiles(w):
        return w.reshape(L1_TILES, 3 * FIELDS, H1).transpose(1, 0, 2)

    def hidden(v):
        return v.reshape(HID_T, HID_K).T

    ow = a["out_w"]
    cuts = [0, 1, 1 + NEXT, 1 + NEXT + H2, 1 + NEXT + H2 + HIDDEN]
    ow_lin, ow_hi, ow_h2, ow_y = (ow[cuts[n]:cuts[n + 1]] for n in range(4))
    sent = {
        "idx": a["r_feat_index"], "emb": a["emb_table"],
        "lin_w": a["linear_w"].reshape(FLAT_T, FLAT_K).T, "lin_b": a["linear_b"].reshape(1, 1),
        "w1a": tiles(fwd), "w1b": tiles(bwd), "b1": a["conv_b1"].reshape(H1, 1),
        "w2": a["conv_w2"].transpose(2, 1, 0).reshape(FIELDS * NEXT, H2), "b2": a["conv_b2"].reshape(H2, 1),
        "dw1": a["deep_w1"], "db1": hidden(a["deep_b1"]), "g1": hidden(a["bn_g1"]), "be1": hidden(a["bn_b1"]),
        "dw2": a["deep_w2"], "db2": hidden(a["deep_b2"]), "g2": hidden(a["bn_g2"]), "be2": hidden(a["bn_b2"]),
        "ow_lin": ow_lin, "ow_hi": ow_hi, "ow_h2": ow_h2, "ow_y": hidden(ow_y), "ob": a["out_b"].reshape(1, 1),
    }
    nc = _bacc.Bacc("TRN2", target_bir_lowering=False, num_devices=1)
    arrays, args = {}, []
    for name, v in sent.items():
        v = _np.ascontiguousarray(v)
        arrays[f"in_{name}"] = v
        args.append(nc.dram_tensor(f"in_{name}", v.shape, _mybir.dt.from_np(v.dtype), kind="ExternalInput").ap())
    out = nc.dram_tensor("out_y", (BATCH, 1), _mybir.dt.float32, kind="ExternalOutput").ap()
    build(nc, *args, out)
    r = _run(nc, [arrays], core_ids=[0])
    return r.results[0]["out_y"]
```

```python
import concourse.bass as bass
from concourse import mybir
from contextlib import ExitStack


BATCH, FIELDS, DIM, VOCAB = 512, 39, 16, 125000
H1, H2 = 128, 128
NEXT = H1 // 2
HIDDEN = 400
BN_EPS = 1e-5

ROWS = 64
BLOCKS = BATCH // ROWS
TOK = DIM * ROWS
BANK = 512
CHUNKS = TOK // BANK
HALF_F = (FIELDS + 1) // 2
FLAT_FIELDS = [7, 7, 6]
FLAT_ROWS = [DIM * n for n in FLAT_FIELDS]
FLAT_TILES = [(q, half, DIM * min(n, FIELDS - HALF_F * half - 7 * q))
              for half in range(2) for q, n in enumerate(FLAT_FIELDS)]

OFFSETS = [[3 * t + 1, 3 * t + 2, 3 * t + 3] for t in range(6)] + [[0, 19]]
L1_TILES = len(OFFSETS)
L2_PAIRS = FIELDS // 2
TAIL = L2_PAIRS
L2_ORDER = [1, TAIL, 0] + [t for n in range(2, L2_PAIRS - 1, 2) for t in (n + 1, n)] + [L2_PAIRS - 1]
L2_TILES = len(L2_ORDER)
PER_STEP = L1_TILES + L2_TILES
RING = 9
SPLIT_RING = 7

L1_SPLIT = [1, 5]
L2_SPLIT = [TAIL, 0, 2, 4, 6, 8, 10, 12, 13, 14, 16, 18]
POOL_LOW = {1: [1, 5], 2: [2, 6, 10, 12, 16]}
FIRST_SPLIT = [TAIL, 0, 4, 8, 10, 12, 14, 16, 18]
FIRST_POOL_LOW = [10, 14, 18]
LAST_WHOLE = {1: [0, 4, 6], 2: [1, 3, 7, 11, 15, 17]}
LAST_POOL_LOW = {1: [1, 3, 5], 2: [0, 2, 4, 6, 8, 10, 12, 14, 16]}
SPLITS_PER_STEP = len(L1_SPLIT) + len(L2_SPLIT)
assert PER_STEP % RING == 0 and SPLITS_PER_STEP % SPLIT_RING == 0


L1_SEQ = [(1, t) for t in range(L1_TILES)]
L2_SEQ = [(2, t) for t in L2_ORDER]
SEQ = L1_SEQ + L2_SEQ + L1_SEQ + (L1_SEQ + L2_SEQ) * (BLOCKS - 2) + L2_SEQ

HID_K = 100
HID_T = HIDDEN // HID_K


def first_of_l1(j):
    return [0, PER_STEP][j] if j < 2 else PER_STEP + L1_TILES + PER_STEP * (j - 2)


def first_of_l2(j):
    return L1_TILES if j == 0 else first_of_l1(j + 1) + (L1_TILES if j < BLOCKS - 1 else 0)


LAST_FROM = first_of_l2(BLOCKS - 3)


def is_split(s):
    layer, t = SEQ[s]
    if L1_TILES <= s < PER_STEP:
        return t in FIRST_SPLIT
    if s >= LAST_FROM:
        return t not in LAST_WHOLE[layer]
    return t in (L1_SPLIT if layer == 1 else L2_SPLIT)


def rows_of(tile):
    layer, t = tile
    return FIELDS * len(OFFSETS[t]) if layer == 1 else NEXT if t == TAIL else 128


def splits_before(s):
    return sum(is_split(r) for r in range(s))


def on_pool(s):
    layer, t = SEQ[s]
    if s < PER_STEP:
        return layer == 2 and t in FIRST_POOL_LOW
    if s >= LAST_FROM:
        return t in LAST_POOL_LOW[layer]
    return t in POOL_LOW[layer]


def loads_landed(s):
    return 16 * (s // RING + 1)


def build(nc, idx, emb, lin_w, lin_b, w1a, w1b, b1, w2, b2, dw1, db1, g1, be1, dw2, db2, g2, be2,
          ow_lin, ow_hi, ow_h2, ow_y, ob, out):
    F32, F32R, I32 = mybir.dt.float32, mybir.dt.float32r, mybir.dt.int32
    ALU, ACT, AX = mybir.AluOpType, mybir.ActivationFunctionType, mybir.AxisListType

    xs = nc.dram_tensor("xs_scratch", [BLOCKS * 2 * FIELDS, TOK], F32).ap()

    def xs_rows(row, groups, group_stride, n, row_stride):
        return bass.AP(xs.tensor, row * TOK, [[group_stride * TOK, groups], [row_stride * TOK, n], [1, TOK]])

    ctx = ExitStack()
    with ctx:
        def sb(name, shape, dt=F32):
            return ctx.enter_context(nc.sbuf_tensor(name, shape, dt))

        def ps(name, shape, dt=F32):
            return ctx.enter_context(nc.psum_tensor(name, shape, dt))

        def sem(name):
            return ctx.enter_context(nc.semaphore(name))

        idx_raw = sb("idx_raw", [128, BLOCKS, HALF_F], I32)
        idx_wrap = sb("idx_wrap", [128, BLOCKS, HALF_F], F32)
        idx_all = sb("idx_all", [128, BLOCKS, HALF_F], I32)
        idx_cur = sb("idx_cur", [128, HALF_F], I32)
        G = sb("G", [128, HALF_F * DIM])
        ident = sb("ident", [128, 128])
        flatT = sb("flatT", [FLAT_ROWS[0], len(FLAT_FIELDS), 2, BATCH])
        xT = sb("xT", [FLAT_ROWS[0], len(FLAT_FIELDS), 2, ROWS])
        ring = sb("ring", [128, RING, TOK])
        zh = sb("zh", [128, SPLIT_RING, TOK], F32R)
        zl = sb("zl", [128, SPLIT_RING, TOK], F32R)
        xa = sb("xa", [3 * FIELDS, TOK])
        xa_block1 = sb("xa_block1", [3 * FIELDS, TOK])
        hi = sb("hi", [128, TOK])
        h2s = sb("h2s", [128, TOK])
        hi_sum = sb("hi_sum", [128, BATCH])
        h2_sum = sb("h2_sum", [128, BATCH])
        w1s = sb("w1s", [3 * FIELDS, L1_TILES, H1])
        w1b_sb = sb("w1b_sb", [3 * FIELDS, L1_TILES, H1])
        w2s = sb("w2s", [128, L2_TILES, H2])
        w1h = sb("w1h", [3 * FIELDS, L1_TILES, H1], F32R)
        w1l = sb("w1l", [3 * FIELDS, L1_TILES, H1], F32R)
        w2h = sb("w2h", [128, L2_TILES, H2], F32R)
        w2l = sb("w2l", [128, L2_TILES, H2], F32R)
        b1_sb = sb("b1_sb", [H1, 1])
        b1_dup = sb("b1_dup", [128, 1])
        b2_sb = sb("b2_sb", [H2, 1])
        dw1_sb = sb("dw1_sb", [FLAT_ROWS[0], len(FLAT_TILES), HIDDEN + 1])
        dw2_sb = sb("dw2_sb", [HID_K, HID_T, HIDDEN])
        vec = sb("vec", [HID_K, 6, HID_T])
        lb_sb = sb("lb_sb", [HID_K + 1, 1])
        pre = sb("pre", [HID_K, HID_T, BATCH])
        act = sb("act", [HID_K + 1, HID_T, BATCH])
        stats = sb("stats", [HID_K, HID_T, 6])
        mv = sb("mv", [HID_K, HID_T, 2])
        bn = sb("bn", [HID_K, 8, HID_T])
        scale = sb("scale", [HID_K, 2, HID_T])
        shift = sb("shift", [HID_K, 2, HID_T])
        ow_hi_sb = sb("ow_hi_sb", [128, 1])
        ow_h2_sb = sb("ow_h2_sb", [H2, 1])
        ow_y_sb = sb("ow_y_sb", [HID_K + 1, HID_T])
        ob_sb = sb("ob_sb", [1, 1])
        res = sb("res", [1, BATCH])

        p_h1 = ps("p_h1", [H1, TOK])
        p_h2 = ps("p_h2", [H2, TOK])
        p_n = ps("p_n", [128, TOK])
        p_t = ps("p_t", [128, BANK])
        p_e = ps("p_e", [128, BANK])
        p_d = [p_e, p_t]

        s_idx = sem("s_idx")
        s_clamp = sem("s_clamp")
        s_w = sem("s_w")
        s_small = sem("s_small")
        s_ident = sem("s_ident")
        s_cur = sem("s_cur")
        s_gather = sem("s_gather")
        s_zero = sem("s_zero")
        s_sym = sem("s_sym")
        s_wh = sem("s_wh")
        s_wl = sem("s_wl")
        s_tp = sem("s_tp")
        s_xs = sem("s_xs")
        s_load = [sem(f"s_load{r}") for r in range(RING)]
        s_xa = sem("s_xa")
        s_xa_block1 = sem("s_xa_block1")
        s_xa_free = sem("s_xa_free")
        s_z = sem("s_z")
        s_zh = sem("s_zh")
        s_free = [sem(f"s_free{r}") for r in range(RING)]
        s_parts = sem("s_parts")
        s_n = sem("s_n")
        s_n_free = sem("s_n_free")
        s_x = sem("s_x")
        s_l1 = sem("s_l1")
        s_l2 = sem("s_l2")
        s_hi = sem("s_hi")
        s_hi_sum = sem("s_hi_sum")
        s_h2 = sem("s_h2")
        s_h2_sum = sem("s_h2_sum")
        s_te = sem("s_te")
        s_deep = sem("s_deep")
        s_pre = sem("s_pre")
        s_bn = sem("s_bn")
        s_eps = sem("s_eps")
        s_root = sem("s_root")
        s_coef = sem("s_coef")
        s_act = sem("s_act")
        s_lin = sem("s_lin")
        s_acc = sem("s_acc")
        s_res = sem("s_res")
        s_out = sem("s_out")

        s_past = sem("s_past")

        def own_wait(eng, semaphore, value):
            eng.wait_ge(semaphore, value)
            eng.sem_inc(s_past, 1)

        def fields_of(j):
            return xa_block1 if j == 1 else xa

        block = ctx.enter_context(nc.Block())

        weight_parts = [(w1h[:, 0:6, :], w1l[:, 0:6, :], w1s[:, 0:6, :]),
                        (w1h[0:78, 6, :], w1l[0:78, 6, :], w1s[0:78, 6, :]),
                        (w2h[:, :, :], w2l[:, :, :], w2s[:, :, :])]
        XS_PARTS = [[(0, None, 7), (1, None, 7), (2, 0, 6), (2, 1, 5)], [(0, 0, 7), (1, 0, 7), (2, 0, 5)]]
        XS_WRITES = sum(map(len, XS_PARTS))
        XS_AT = 17
        SMALL = 16 * (4 + 2 * len(FLAT_TILES) + 1 + 6 + 6)

        LAG = 5
        T_AT = 6
        T0_AT = 10
        GATHERS_AHEAD, GATHERS_L1 = 13, 19
        LOW_BEHIND = 2
        H1_SUM = 3
        HI_OUT = 8
        H2_OUT, H2_SUM = 2, 13
        S5, S6, S7 = BLOCKS - 3, BLOCKS - 2, BLOCKS - 1
        DEEP1_AT = [(S5, 2, 12), (S5, 2, 16), (S6, 1, 1), (S6, 1, 5)]
        BIAS1_AT = [(S5, 2, 18), (S6, 1, 2), (S6, 2, 0), (S6, 2, 4)]
        STAT1_AT = [(S5, 2, 19), (S6, 1, 3), (S6, 2, 1), (S6, 2, 5)]
        EPS1_AT, ROOT1_AT, COEF1_AT, ACT1_AT = (S6, 2, 6), (S6, 2, 6), (S6, 2, 7), (S6, 2, 8)
        DEEP2_AT = [(S6, 2, 7), (S6, 2, 10), (S6, 2, 13), (S6, 2, 16)]
        BIAS2_AT = [(S6, 2, 12), (S6, 2, 15), (S6, 2, 18), (S7, 2, 1)]
        STAT2_AT = [(S6, 2, 13), (S6, 2, 16), (S6, 2, 19), (S7, 2, 2)]
        EPS2_AT, ROOT2_AT, COEF2_AT, ACT2_AT = (S7, 2, 3), (S7, 2, 3), (S7, 2, 4), (S7, 2, 4)
        TOTAL_AT = (S7, 2, 15)

        def deep_work(j, layer, *works):
            return [(at[2], work) for at, work in works if at[:2] == (j, layer)]

        def steps(eng, step):
            with eng.Fori(0, BLOCKS - 4) as k:
                step(1, k)
            for j in range(BLOCKS - 3, BLOCKS):
                step(j, 0)

        @block.sync
        def _(sp):
            sp.dma_start(idx_raw[:, :, :], idx).then_inc(s_idx, 16)
            sp.dma_start(w1s[:, 0:6, :], w1a[:, 0:6, :]).then_inc(s_w, 16)
            sp.dma_start(w1s[0:78, 6, :], w1a[0:78, 6, :]).then_inc(s_w, 16)
            sp.dma_start(w1b_sb[:, 0:6, :], w1b[:, 0:6, :]).then_inc(s_w, 16)
            sp.dma_start(w1b_sb[FIELDS:2 * FIELDS, 6, :], w1b[FIELDS:2 * FIELDS, 6, :]).then_inc(s_w, 16)
            sp.dma_start(w2s[:, 0:L2_PAIRS, :], w2[0:128 * L2_PAIRS, :].rearrange("(t p) o -> p t o", p=128)).then_inc(s_w, 16)
            for half in range(2):
                sp.dma_start(w2s[NEXT * half:NEXT * (half + 1), TAIL, :], w2[128 * L2_PAIRS:, :]).then_inc(s_w, 16)
            sp.dma_start(b1_sb[:, :], b1).then_inc(s_small, 16)
            for half in range(2):
                sp.dma_start(b1_dup[NEXT * half:NEXT * (half + 1), :], b1[0:NEXT, :]).then_inc(s_small, 16)
            sp.dma_start(b2_sb[:, :], b2).then_inc(s_small, 16)
            row = 0
            for n, (_, _, r) in enumerate(FLAT_TILES):
                sp.dma_start(dw1_sb[0:r, n, 0:HIDDEN], dw1[row:row + r, :]).then_inc(s_small, 16)
                sp.dma_start(dw1_sb[0:r, n, HIDDEN:], lin_w[row:row + r, :]).then_inc(s_small, 16)
                row += r
            sp.dma_start(dw2_sb[:, :, :], dw2.rearrange("(t p) o -> p t o", p=HID_K)).then_inc(s_small, 16)
            for n, v in enumerate((db1, g1, be1, db2, g2, be2)):
                sp.dma_start(vec[:, n, :], v).then_inc(s_small, 16)
            sp.wait_ge(s_zero, 2)
            for dst, src in ((lb_sb[HID_K:, :], lin_b), (ow_y_sb[HID_K:, HID_T - 1:], ow_lin),
                             (ow_y_sb[0:HID_K, :], ow_y), (ow_h2_sb[:, :], ow_h2), (ob_sb[:, :], ob)):
                sp.dma_start(dst, src).then_inc(s_small, 16)
            sp.dma_start(ow_hi_sb[NEXT:128, :], ow_hi).then_inc(s_small, 16)

            def write_scratch(j, k):
                own_wait(sp, s_x, len(FLAT_ROWS) * (j + 1) + len(FLAT_ROWS) * k)
                for copy in range(2):
                    for q, half, fields in XS_PARTS[copy]:
                        halves = 2 if half is None else 1
                        half = half or 0
                        row = (j + k) * 2 * FIELDS + FIELDS * copy + 7 * q + HALF_F * half
                        dst = bass.AP(xs.tensor, row * TOK, [[ROWS, DIM * fields], [HALF_F * TOK, halves], [1, ROWS]])
                        sp.dma_start(dst, xT[0:DIM * fields, q, half:half + halves, :]).then_inc(s_xs, 16)

            def load_tiles(j, k, layer, writes={}):
                row = (j + k) * 2 * FIELDS
                if layer == 1:
                    own_wait(sp, s_xs, 16 * XS_WRITES * (j + 1 + k))
                    if j != 1:
                        own_wait(sp, s_xa_free, max(j, 1) + k)
                    sp.dma_start(fields_of(j)[:, :], xs_rows(row, 3, 0, FIELDS, 1)).then_inc(s_xa_block1 if j == 1 else s_xa, 16)
                seq0 = first_of_l1(j) if layer == 1 else first_of_l2(j)
                for n, (_, t) in enumerate(L1_SEQ if layer == 1 else L2_SEQ):
                    s = seq0 + n
                    slot = s % RING
                    if s >= RING:
                        own_wait(sp, s_free[slot], s // RING + PER_STEP // RING * k)
                    if layer == 1:
                        offs = OFFSETS[t]
                        rows = xs_rows(row + offs[0], len(offs), offs[1] - offs[0], FIELDS, 1)
                    else:
                        rows = xs_rows(row + 2 * t, 1 if t == TAIL else 2, 1, NEXT, 0)
                    sp.dma_start(ring[0:rows_of((layer, t)), slot, :], rows).then_inc(s_load[slot], 16)
                    if n in writes:
                        write_scratch(writes[n], k)

            write_scratch(0, 0)
            load_tiles(0, 0, 1)
            load_tiles(0, 0, 2, {6: 1, L2_TILES - 1: 2})
            load_tiles(1, 0, 1)

            def step(j, k):
                if j + 1 < BLOCKS:
                    load_tiles(j + 1, k, 1)
                load_tiles(j, k, 2, {XS_AT: j + 2} if j < BLOCKS - 2 else {})

            steps(sp, step)

            sp.wait_ge(s_res, 1)
            sp.dma_start(out.rearrange("b o -> o b"), res[:, :]).then_inc(s_out, 16)
            sp.wait_ge(s_out, 16)

        @block.gpsimd
        def _(pool):
            def indices(j, k):
                if j:
                    own_wait(pool, s_tp, j + k)
                nc.gpsimd.tensor_copy(idx_cur[:, :], idx_all[:, bass.ds(j + k, 1), :].rearrange("p a f -> p (a f)")).then_inc(s_cur, 1)
                own_wait(pool, s_cur, j + 1 + k)

            def gather(fields):
                for f in fields:
                    nc.gpsimd.indirect_dma_start(
                        G[:, DIM * f:DIM * (f + 1)], None, emb[:, :],
                        bass.IndirectOffsetOnAxis(idx_cur[:, f:f + 1], 0)).then_inc(s_gather, 16)

            def low_part(s, k):
                q = splits_before(s)
                own_wait(pool, s_zh, q + 1 + SPLITS_PER_STEP * k)
                slot, part, r = s % RING, q % SPLIT_RING, rows_of(SEQ[s])
                nc.gpsimd.tensor_tensor(zl[0:r, part, :], ring[0:r, slot, :],
                                        zh[0:r, part, :].bitcast(F32), ALU.subtract).then_inc(s_free[slot], 1)

            def low_parts(j, k, layer, lows, fields=()):
                seq0 = first_of_l1(j) if layer == 1 else first_of_l2(j)
                for m, t in enumerate(lows):
                    low_part(seq0 + (L1_SEQ if layer == 1 else L2_SEQ).index((layer, t)), k)
                    gather(fields[len(fields) * m // len(lows):len(fields) * (m + 1) // len(lows)])

            low1, low2 = POOL_LOW[1], POOL_LOW[2]
            all_fields = list(range(HALF_F))
            ahead, then, rest = all_fields[:GATHERS_AHEAD], all_fields[GATHERS_AHEAD:GATHERS_L1], all_fields[GATHERS_L1:]

            pool.wait_ge(s_clamp, 3)
            indices(0, 0)
            gather(range(HALF_F))
            nc.gpsimd.memset(ident[:, :], 0.0).then_inc(s_ident, 1)
            pool.wait_ge(s_ident, 1)
            nc.gpsimd.affine_select(out=ident[:, :], in_=ident[:, :], compare_op=ALU.not_equal, fill=1.0,
                                    base=0, pattern=[[-1, 128]], channel_multiplier=1).then_inc(s_ident, 1)
            indices(1, 0)
            gather(all_fields)
            indices(2, 0)
            gather(all_fields)
            low_parts(0, 0, 2, FIRST_POOL_LOW[:1])
            indices(3, 0)
            low_parts(0, 0, 2, FIRST_POOL_LOW[1:], ahead[:4])
            low_parts(1, 0, 1, low1, ahead[4:])

            def step(j, k):
                if j >= BLOCKS - 2:
                    if j + 1 < BLOCKS:
                        low_parts(j + 1, k, 1, LAST_POOL_LOW[1])
                    low_parts(j, k, 2, LAST_POOL_LOW[2])
                    return
                low_parts(j + 1, k, 1, low1, then)
                if j == BLOCKS - 3:
                    gather(rest)
                    low_parts(j, k, 2, LAST_POOL_LOW[2])
                    return
                low_parts(j, k, 2, low2[:1], rest)
                low_parts(j, k, 2, low2[1:2])
                indices(j + 3, k)
                gather(ahead[:3])
                low_parts(j, k, 2, low2[2:], ahead[3:])

            steps(pool, step)

        @block.vector
        def _(dve):
            nc.vector.sem_inc(s_xa_free, 1)
            dve.wait_ge(s_idx, 16)
            nc.vector.tensor_scalar(idx_wrap[:, :, :], idx_raw[:, :, :], 0.0, float(VOCAB), ALU.is_lt, ALU.mult).then_inc(s_clamp, 1)
            dve.wait_ge(s_clamp, 1)
            nc.vector.tensor_tensor(idx_wrap[:, :, :], idx_wrap[:, :, :], idx_raw[:, :, :], ALU.add).then_inc(s_clamp, 1)
            dve.wait_ge(s_clamp, 2)
            nc.vector.tensor_scalar(idx_all[:, :, :], idx_wrap[:, :, :], 0.0, float(VOCAB - 1), ALU.max, ALU.min).then_inc(s_clamp, 1)

            nc.vector.memset(w1b_sb[0:FIELDS, 6, :], 0.0).then_inc(s_zero, 1)
            nc.vector.memset(lb_sb[96:, :], 0.0).then_inc(s_zero, 1)
            dve.wait_ge(s_zero, 2)
            dve.wait_ge(s_w, 7 * 16)
            nc.vector.tensor_tensor(w1s[:, 0:6, :], w1s[:, 0:6, :], w1b_sb[:, 0:6, :], ALU.add).then_inc(s_sym, 1)
            nc.vector.tensor_tensor(w1s[0:78, 6, :], w1s[0:78, 6, :], w1b_sb[0:78, 6, :], ALU.add).then_inc(s_sym, 1)
            dve.wait_ge(s_wh, 1)
            dve.wait_ge(s_sym, 2)
            for high, low, whole in weight_parts:
                last = nc.vector.tensor_tensor(low, whole, high.bitcast(F32), ALU.subtract)
            last.then_inc(s_wl, 1)

            def low_part(s, k):
                q = splits_before(s)
                dve.wait_ge(s_zh, q + 1 + SPLITS_PER_STEP * k)
                slot, part, r = s % RING, q % SPLIT_RING, rows_of(SEQ[s])
                if SEQ[s] == (2, TAIL):
                    nc.vector.tensor_tensor(zh[NEXT:128, part, :], ring[0:NEXT, slot, :],
                                            zh[0:NEXT, part, :].bitcast(F32), ALU.subtract).then_inc(s_free[slot], 1)
                else:
                    nc.vector.tensor_tensor(zl[0:r, part, :], ring[0:r, slot, :],
                                            zh[0:r, part, :].bitcast(F32), ALU.subtract).then_inc(s_free[slot], 1)

            def products(j, k, layer, extras=()):
                if layer == 1:
                    if j == 1:
                        dve.wait_ge(s_xa_block1, 16)
                    else:
                        dve.wait_ge(s_xa, 16 * max(j, 1) + 16 * k)
                else:
                    dve.wait_ge(s_n, j + 1 + k)
                seq0 = first_of_l1(j) if layer == 1 else first_of_l2(j)
                tiles = L1_SEQ if layer == 1 else L2_SEQ
                for n, tile in enumerate(tiles):
                    s = seq0 + n
                    slot, r = s % RING, rows_of(tile)
                    dve.wait_ge(s_load[slot], loads_landed(s) + 16 * PER_STEP // RING * k)
                    by = (fields_of(j) if layer == 1 else p_n)[0:r, :]
                    nc.vector.tensor_tensor(ring[0:r, slot, :], by, ring[0:r, slot, :], ALU.mult).then_inc(s_z, 1)
                    if n >= LOW_BEHIND and is_split(s - LOW_BEHIND) and not on_pool(s - LOW_BEHIND):
                        low_part(s - LOW_BEHIND, k)
                    for work in [w for at, w in extras if at == n]:
                        work()
                for s in range(seq0 + len(tiles) - LOW_BEHIND, seq0 + len(tiles)):
                    if is_split(s) and not on_pool(s):
                        low_part(s, k)
                dve.wait_ge(s_z, seq0 + len(tiles) + PER_STEP * k)
                if layer == 2:
                    nc.vector.sem_inc(s_n_free, 1)
                elif j != 1:
                    nc.vector.sem_inc(s_xa_free, 1)

            def sum_d(dst, src, j, k):
                return nc.vector.tensor_reduce(dst[:, bass.ds(ROWS * j + ROWS * k, ROWS)],
                                               src.rearrange("p (d b) -> p b d", d=DIM), AX.X, ALU.add)

            def sum_h2(j, k):
                dve.wait_ge(s_h2, j + 1 + k)
                sum_d(h2_sum[:, :], h2s[:, :], j, k).then_inc(s_h2_sum, 1)

            def sum_hi(j, k):
                dve.wait_ge(s_hi, j + 1 + k)
                sum_d(hi_sum[NEXT:128, :], hi[NEXT:128, :], j, k).then_inc(s_hi_sum, 1)

            count = [0]

            def chain(ins):
                count[0] += 1
                ins.then_inc(s_bn, 1)
                dve.wait_ge(s_bn, count[0])

            def statistics(layer, t):
                dve.wait_ge(s_pre, layer * HID_T + t + 1)
                chain(nc.vector.bn_stats(stats[:, t, :], pre[:, t, :]))
                chain(nc.vector.bn_aggr(mv[:, t, :], stats[:, t, :]))

            def add_eps(layer):
                nc.vector.tensor_scalar(bn[:, 0, :], mv[:, :, 1], BN_EPS, None, ALU.add).then_inc(s_eps, 1)

            def coefficients(layer):
                dve.wait_ge(s_root, layer + 1)
                chain(nc.vector.reciprocal(bn[:, 2, :], bn[:, 1, :]))
                chain(nc.vector.tensor_tensor(bn[:, 3, :], bn[:, 0, :], bn[:, 2, :], ALU.mult))
                chain(nc.vector.tensor_tensor(bn[:, 4, :], bn[:, 3, :], bn[:, 1, :], ALU.add))
                chain(nc.vector.tensor_scalar(bn[:, 5, :], bn[:, 4, :], 0.5, None, ALU.mult))
                chain(nc.vector.reciprocal(bn[:, 6, :], bn[:, 5, :]))
                chain(nc.vector.tensor_tensor(scale[:, layer, :], bn[:, 6, :], vec[:, 3 * layer + 1, :], ALU.mult))
                chain(nc.vector.tensor_tensor(bn[:, 7, :], mv[:, :, 0], scale[:, layer, :], ALU.mult))
                nc.vector.tensor_tensor(shift[:, layer, :], vec[:, 3 * layer + 2, :], bn[:, 7, :], ALU.subtract).then_inc(s_coef, 1)

            products(0, 0, 1)
            products(0, 0, 2, [(H1_SUM, lambda: sum_hi(0, 0))])
            products(1, 0, 1)

            works = [(at, lambda t=t: statistics(0, t)) for t, at in enumerate(STAT1_AT)]
            works += [(EPS1_AT, lambda: add_eps(0)), (COEF1_AT, lambda: (dve.wait_ge(s_small, SMALL), coefficients(0)))]
            works += [(at, lambda t=t: statistics(1, t)) for t, at in enumerate(STAT2_AT)]
            works += [(EPS2_AT, lambda: add_eps(1)), (COEF2_AT, lambda: coefficients(1))]

            def step(j, k):
                if j + 1 < BLOCKS:
                    products(j + 1, k, 1, deep_work(j, 1, *works))
                products(j, k, 2, [(H1_SUM, lambda: sum_hi(j, k)), (H2_SUM, lambda: sum_h2(j - 1, k))] + deep_work(j, 2, *works))

            steps(dve, step)
            sum_h2(BLOCKS - 1, 0)

        @block.tensor
        def _(pe):
            def transposes(j, k):
                own_wait(pe, s_gather, 16 * HALF_F * (j + 1 + k))
                if j:
                    own_wait(pe, s_te, j + k)
                for q, r in enumerate(FLAT_ROWS):
                    last = nc.tensor.transpose(p_t[0:r, 128 * q:128 * (q + 1)],
                                               G[:, FLAT_ROWS[0] * q:FLAT_ROWS[0] * q + r], ident[:, :])
                last.then_inc(s_tp, 1)

            def contract(j, k, layer, extras=()):
                acc = p_h1 if layer == 1 else p_h2
                seq0 = first_of_l1(j) if layer == 1 else first_of_l2(j)
                tiles = L1_SEQ if layer == 1 else L2_SEQ
                if j:
                    if layer == 1:
                        pe.wait_ge(s_hi, j + k)
                        pe.wait_ge(s_n, j + k)
                    else:
                        pe.wait_ge(s_h2, j + k)
                for n, tile in enumerate(tiles):
                    s = seq0 + n
                    t, slot, r = tile[1], s % RING, rows_of(tile)
                    first, final = n == 0, n == len(tiles) - 1

                    def mm(c, w, x, start=False, stop=False):
                        return nc.tensor.matmul(acc[:, BANK * c:BANK * (c + 1)], w, x[:, BANK * c:BANK * (c + 1)],
                                                start=start, stop=stop)

                    if not is_split(s):
                        pe.wait_ge(s_z, s + 1 + PER_STEP * k)
                        w = (w1s if layer == 1 else w2s)[0:r, t, :]
                        for c in range(CHUNKS):
                            last = mm(c, w, ring[0:r, slot, :], first, final)
                    else:
                        q = splits_before(s)
                        part = q % SPLIT_RING
                        wh, wl = ((w1h, w1l) if layer == 1 else (w2h, w2l))
                        wh, wl = wh[0:r, t, :], wl[0:r, t, :]
                        high, low = zh[0:r, part, :], zl[0:r, part, :]
                        if layer == 2 and t == TAIL:
                            wh, wl, high = w2h[:, t, :], w2l[:, t, :], zh[:, part, :]
                            pe.wait_ge(s_free[slot], s // RING + 1 + PER_STEP // RING * k)
                            for c in range(CHUNKS):
                                mm(c, wl, high, first)
                            for c in range(CHUNKS):
                                last = mm(c, wh, high, False, final)
                        else:
                            pe.wait_ge(s_zh, q + 1 + SPLITS_PER_STEP * k)
                            for c in range(CHUNKS):
                                mm(c, wl, high, first)
                            for c in range(CHUNKS):
                                mm(c, wh, high)
                            pe.wait_ge(s_free[slot], s // RING + 1 + PER_STEP // RING * k)
                            for c in range(CHUNKS):
                                last = mm(c, wh, low, False, final)
                    last.then_inc(s_parts if is_split(s) else s_free[slot], 1)
                    for work in [w for at, w in extras if at == n]:
                        work()
                if is_split(s):
                    own_wait(pe, s_parts, splits_before(s) + 1 + SPLITS_PER_STEP * k)
                else:
                    own_wait(pe, s_free[slot], s // RING + 1 + PER_STEP // RING * k)
                nc.tensor.sem_inc(s_l1 if layer == 1 else s_l2, 1)

            def deep(layer, t):
                n = layer * HID_T + t
                if n == 0:
                    pe.wait_ge(s_te, BLOCKS)
                    pe.wait_ge(s_small, SMALL)
                if n >= 2:
                    pe.wait_ge(s_pre, n - 1)
                if n == HID_T - 1 + 2:
                    pe.wait_ge(s_lin, 1)
                if layer == 0:
                    parts = [(dw1_sb[0:r, c, :], flatT[0:r, q, half, :]) for c, (q, half, r) in enumerate(FLAT_TILES)]
                else:
                    pe.wait_ge(s_act, HID_T)
                    parts = [(dw2_sb[:, c, :], act[0:HID_K, c, :]) for c in range(HID_T)]
                end = HIDDEN + 1 if n == HID_T - 1 else HID_K * (t + 1)
                for c, (w, x) in enumerate(parts):
                    last = nc.tensor.matmul(p_d[n % 2][0:end - HID_K * t, :], w[:, HID_K * t:end], x,
                                            start=c == 0, stop=c == len(parts) - 1)
                last.then_inc(s_deep, 1)

            total = p_h1[0:1, 0:BANK]

            def total_begin():
                pe.wait_ge(s_hi_sum, BLOCKS)
                nc.tensor.matmul(total, ow_hi_sb[NEXT:128, :], hi_sum[NEXT:128, :], start=True, stop=False)
                pe.wait_ge(s_act, 2 * HID_T)
                for t in range(HID_T):
                    r = HID_K if t < HID_T - 1 else HID_K + 1
                    nc.tensor.matmul(total, ow_y_sb[0:r, t:t + 1], act[0:r, t, :], start=False, stop=False)

            pe.wait_ge(s_ident, 2)
            transposes(0, 0)
            pe.wait_ge(s_wl, 1)
            contract(0, 0, 1)
            transposes(1, 0)
            contract(0, 0, 2, [(T0_AT, lambda: transposes(2, 0))])
            contract(1, 0, 1)

            works = [(at, lambda t=t: deep(0, t)) for t, at in enumerate(DEEP1_AT)]
            works += [(at, lambda t=t: deep(1, t)) for t, at in enumerate(DEEP2_AT)]
            works += [(TOTAL_AT, total_begin)]

            def step(j, k):
                if j + 1 < BLOCKS:
                    contract(j + 1, k, 1, deep_work(j, 1, *works))
                contract(j, k, 2, ([(T_AT, lambda: transposes(j + 2, k))] if j < BLOCKS - 2 else []) + deep_work(j, 2, *works))

            steps(pe, step)

            pe.wait_ge(s_h2_sum, BLOCKS)
            nc.tensor.matmul(total, ow_h2_sb[:, :], h2_sum[:, :], start=False, stop=True).then_inc(s_acc, 1)

        @block.scalar
        def _(sc):
            sc.wait_ge(s_sym, 2)
            for high, _, whole in weight_parts:
                last = nc.scalar.activation(high, whole, ACT.Copy)
            last.then_inc(s_wh, 1)

            def out_of_transposes(j, k):
                sc.wait_ge(s_tp, j + 1 + k)
                if j:
                    sc.wait_ge(s_xs, 16 * XS_WRITES * j + 16 * XS_WRITES * k)
                for q, r in enumerate(FLAT_ROWS):
                    nc.scalar.activation(xT[0:r, q, :, :].rearrange("p a b -> p (a b)"), p_t[0:r, 128 * q:128 * (q + 1)],
                                         ACT.Copy).then_inc(s_x, 1)
                for q, r in enumerate(FLAT_ROWS):
                    last = nc.scalar.activation(flatT[0:r, q, :, bass.ds(ROWS * j + ROWS * k, ROWS)],
                                                p_t[0:r, 128 * q:128 * (q + 1)].rearrange("p (a b) -> p a b", a=2), ACT.Copy)
                last.then_inc(s_te, 1)

            def high_parts(j, k, layer, extras=()):
                seq0 = first_of_l1(j) if layer == 1 else first_of_l2(j)
                for n, tile in enumerate(L1_SEQ if layer == 1 else L2_SEQ):
                    s = seq0 + n
                    if is_split(s):
                        q = splits_before(s)
                        sc.wait_ge(s_z, s + 1 + PER_STEP * k)
                        if q >= SPLIT_RING:
                            sc.wait_ge(s_parts, q - SPLIT_RING + 1 + SPLITS_PER_STEP * k)
                        r = rows_of(tile)
                        nc.scalar.activation(zh[0:r, q % SPLIT_RING, :], ring[0:r, s % RING, :], ACT.Copy).then_inc(s_zh, 1)
                    for work in [w for at, w in extras if at == n]:
                        work()

            def next_out_of_l1(j, k):
                sc.wait_ge(s_l1, j + 1 + k)
                if j:
                    sc.wait_ge(s_n_free, j + k)
                for half in range(2):
                    last = nc.scalar.activation(p_n[NEXT * half:NEXT * (half + 1), :], p_h1[0:NEXT, :], ACT.Relu,
                                                bias=b1_dup[NEXT * half:NEXT * (half + 1), :])
                last.then_inc(s_n, 1)

            def hi_out_of_l1(j, k):
                sc.wait_ge(s_l1, j + 1 + k)
                if j:
                    sc.wait_ge(s_hi_sum, j + k)
                nc.scalar.activation(hi[NEXT:128, :], p_h1[NEXT:128, :], ACT.Relu, bias=b1_sb[NEXT:128, :]).then_inc(s_hi, 1)

            def out_of_l2(j, k):
                sc.wait_ge(s_l2, j + 1 + k)
                if j:
                    sc.wait_ge(s_h2_sum, j + k)
                nc.scalar.activation(h2s[:, :], p_h2[:, :], ACT.Relu, bias=b2_sb[:, :]).then_inc(s_h2, 1)

            def deep_bias(layer, t):
                n = layer * HID_T + t
                sc.wait_ge(s_deep, n + 1)
                if layer:
                    sc.wait_ge(s_act, HID_T)
                nc.scalar.activation(pre[:, t, :], p_d[n % 2][0:HID_K, :], ACT.Identity, bias=vec[:, 3 * layer, t:t + 1]).then_inc(s_pre, 1)
                if n == HID_T - 1:
                    nc.scalar.activation(act[96:HID_K + 1, t, :], p_d[n % 2][96:HID_K + 1, :], ACT.Identity,
                                         bias=lb_sb[96:, :]).then_inc(s_lin, 1)

            def deep_root(layer):
                sc.wait_ge(s_eps, layer + 1)
                nc.scalar.activation(bn[:, 1, :], bn[:, 0, :], ACT.Sqrt).then_inc(s_root, 1)

            def deep_act(layer):
                sc.wait_ge(s_coef, layer + 1)
                if layer:
                    sc.wait_ge(s_deep, 2 * HID_T)
                else:
                    sc.wait_ge(s_lin, 1)
                for t in range(HID_T):
                    nc.scalar.activation(act[0:HID_K, t, :], pre[:, t, :], ACT.Relu, bias=shift[:, layer, t:t + 1],
                                         scale=scale[:, layer, t:t + 1]).then_inc(s_act, 1)

            out_of_transposes(0, 0)
            high_parts(0, 0, 1)
            sc.wait_ge(s_small, SMALL)
            next_out_of_l1(0, 0)
            hi_out_of_l1(0, 0)
            high_parts(0, 0, 2, [(0, lambda: out_of_transposes(1, 0)), (T0_AT + LAG, lambda: out_of_transposes(2, 0))])
            high_parts(1, 0, 1)
            hi_out_of_l1(1, 0)

            works = [(at, lambda t=t: deep_bias(0, t)) for t, at in enumerate(BIAS1_AT)]
            works += [(ROOT1_AT, lambda: deep_root(0)), (ACT1_AT, lambda: deep_act(0))]
            works += [(at, lambda t=t: deep_bias(1, t)) for t, at in enumerate(BIAS2_AT)]
            works += [(ROOT2_AT, lambda: deep_root(1)), (ACT2_AT, lambda: deep_act(1))]

            def step(j, k):
                next_out_of_l1(j, k)
                if j + 1 < BLOCKS:
                    high_parts(j + 1, k, 1, deep_work(j, 1, *works))
                extras = [(H2_OUT, lambda: out_of_l2(j - 1, k))]
                if j + 1 < BLOCKS:
                    extras += [(HI_OUT, lambda: hi_out_of_l1(j + 1, k))]
                if j < BLOCKS - 2:
                    extras += [(T_AT + LAG, lambda: out_of_transposes(j + 2, k))]
                high_parts(j, k, 2, extras + deep_work(j, 2, *works))
                if j == BLOCKS - 1:
                    out_of_l2(j, 0)

            steps(sc, step)
            sc.wait_ge(s_acc, 1)
            nc.scalar.activation(res[:, :], p_h1[0:1, 0:BANK], ACT.Identity, bias=ob_sb[:, :]).then_inc(s_res, 1)


def kernel(**inputs):
    import numpy as _np
    import concourse.bacc as _bacc
    from concourse import mybir as _mybir
    from concourse.bass_utils import run_bass_kernel_spmd as _run

    a = {k.replace("L0_rec_", ""): _np.asarray(v) for k, v in inputs.items()}
    w1 = a["conv_w1"]
    i = _np.arange(FIELDS)
    order = [k for tile in OFFSETS for k in tile]
    fwd = _np.concatenate([w1[:, i, (i + k) % FIELDS].T for k in order] + [w1[:, i, i].T])
    bwd = _np.concatenate([w1[:, (i + k) % FIELDS, i].T for k in order] + [w1[:, i, i].T])

    fields = _np.minimum(_np.arange(2 * HALF_F), FIELDS - 1).reshape(2, HALF_F)
    idx = a["r_feat_index"].reshape(BLOCKS, ROWS, FIELDS)[:, :, fields].transpose(2, 1, 0, 3).reshape(128, BLOCKS, HALF_F)

    def tiles(w):
        return w.reshape(L1_TILES, 3 * FIELDS, H1).transpose(1, 0, 2)

    def hidden(v):
        return v.reshape(HID_T, HID_K).T

    ow = a["out_w"]
    cuts = [0, 1, 1 + NEXT, 1 + NEXT + H2, 1 + NEXT + H2 + HIDDEN]
    ow_lin, ow_hi, ow_h2, ow_y = (ow[cuts[n]:cuts[n + 1]] for n in range(4))
    sent = {
        "idx": idx, "emb": a["emb_table"],
        "lin_w": a["linear_w"], "lin_b": a["linear_b"].reshape(1, 1),
        "w1a": tiles(fwd), "w1b": tiles(bwd), "b1": a["conv_b1"].reshape(H1, 1),
        "w2": a["conv_w2"].transpose(2, 1, 0).reshape(FIELDS * NEXT, H2), "b2": a["conv_b2"].reshape(H2, 1),
        "dw1": a["deep_w1"], "db1": hidden(a["deep_b1"]), "g1": hidden(a["bn_g1"]), "be1": hidden(a["bn_b1"]),
        "dw2": a["deep_w2"], "db2": hidden(a["deep_b2"]), "g2": hidden(a["bn_g2"]), "be2": hidden(a["bn_b2"]),
        "ow_lin": ow_lin, "ow_hi": ow_hi, "ow_h2": ow_h2, "ow_y": hidden(ow_y), "ob": a["out_b"].reshape(1, 1),
    }
    nc = _bacc.Bacc("TRN2", target_bir_lowering=False, num_devices=1)
    arrays, args = {}, []
    for name, v in sent.items():
        v = _np.ascontiguousarray(v)
        arrays[f"in_{name}"] = v
        args.append(nc.dram_tensor(f"in_{name}", v.shape, _mybir.dt.from_np(v.dtype), kind="ExternalInput").ap())
    out = nc.dram_tensor("out_y", (BATCH, 1), _mybir.dt.float32, kind="ExternalOutput").ap()
    build(nc, *args, out)
    r = _run(nc, [arrays], core_ids=[0])
    return r.results[0]["out_y"]
```
